# Optimizing a Trainium2 kernel written in Bass

```python
import numpy as np
import jax
import jax.numpy as jnp

def _softmax(x, axis=-1):
    return jax.nn.softmax(x, axis=axis)

def _gelu(x):
    return jax.nn.gelu(x, approximate=True)

def _silu(x):
    return jax.nn.silu(x)

def _sigmoid(x):
    return jax.nn.sigmoid(x)

def _layernorm(x, axis=-1, eps=1e-05):
    m = jnp.mean(x, axis=axis, keepdims=True)
    v = jnp.var(x, axis=axis, keepdims=True)
    return (x - m) / jnp.sqrt(v + eps)

def _scatter_add(tgt, idx, src, axis=0):
    return tgt.at[idx].add(src)

def _segment_sum(src, seg, n):
    return jax.ops.segment_sum(src, seg, n)
kernel_name = 'mk_adj_preln_d4_adj_r2_51e902'

def setup_inputs(seed: int=0):
    np.random.seed(seed)
    _w = jnp.asarray

    def _rec_inputs():
        import jax
        import jax.numpy as jnp
        _gk = jax.random.key(seed)
        x = 7.22e-05 + 1 * jax.random.normal(jax.random.fold_in(_gk, 1), (32, 256, 256), jnp.float32)
        _a = jax.random.bernoulli(jax.random.fold_in(_gk, 2), 0.0078125, (256, 256))
        _a = jnp.logical_or(_a, jnp.swapaxes(_a, -1, -2))
        _a = jnp.logical_or(_a, jnp.eye(256, dtype=bool))
        adj = _a.astype(jnp.int32)
        return (x, adj)
    x, adj = _rec_inputs()

    def _L0_gnn_setup():
        import jax, jax.numpy as jnp
        import numpy as np
        B, N, D = (8, 1024, 256)
        NEG_SLOPE = 0.2
        key = jax.random.key(seed)
        k1, k2, k3, k4, k5 = jax.random.split(key, 5)
        x = jax.random.normal(k1, (B, N, D), dtype=jnp.float32)
        adj = jax.random.randint(k2, (N, N), 0, 2, dtype=jnp.int32)
        adj = jnp.maximum(adj, jnp.eye(N, dtype=jnp.int32))
        W = jax.random.normal(k3, (D, D), dtype=jnp.float32) * (1.0 / np.sqrt(D))
        a_src = jax.random.normal(k4, (D,), dtype=jnp.float32) * (1.0 / np.sqrt(D))
        a_dst = jax.random.normal(k5, (D,), dtype=jnp.float32) * (1.0 / np.sqrt(D))
        return {'x': x, 'adj': adj, 'W': W, 'a_src': a_src, 'a_dst': a_dst}
    _L0_gnn_all = _L0_gnn_setup()
    _L0_gnn_in = {k: v for k, v in _L0_gnn_all.items() if k in ('W', 'a_src', 'a_dst')}
    del _L0_gnn_all

    def _L1_gnn_setup():
        import jax, jax.numpy as jnp
        import numpy as np
        LEAKY_ALPHA = 0.01
        NEG_INF = -1000000000.0
        LN_EPS = 1e-05

        def _gat_heads(x, adj, W, a):
            O = W.shape[-1]
            Wh = jnp.einsum('bnf,hfo->bhno', x, W)
            f1 = jnp.einsum('bhno,ho->bhn', Wh, a[:, :O])
            f2 = jnp.einsum('bhno,ho->bhn', Wh, a[:, O:])
            e = f1[:, :, :, None] + f2[:, :, None, :]
            e = jnp.where(e > 0, e, LEAKY_ALPHA * e)
            e = jnp.where(adj[None, None] > 0, e, NEG_INF)
            attn = jax.nn.softmax(e, axis=-1)
            return jnp.einsum('bhnm,bhmo->bhno', attn, Wh)
        key = jax.random.key(seed)
        ks = jax.random.split(key, 10)
        B, N, F_in, F_hid, H, F_out, D_ff = (8, 1024, 256, 256, 4, 256, 256)
        s = 0.05
        return {'enc_inputs': jax.random.normal(ks[0], (B, N, F_in), jnp.float32), 'adj': jax.random.randint(ks[1], (N, N), 0, 2, jnp.int32), 'W_heads': jax.random.normal(ks[2], (H, F_in, F_hid), jnp.float32) * s, 'a_heads': jax.random.normal(ks[3], (H, 2 * F_hid), jnp.float32) * s, 'W_out': jax.random.normal(ks[4], (H * F_hid, F_out), jnp.float32) * s, 'a_out': jax.random.normal(ks[5], (2 * F_out,), jnp.float32) * s, 'w1': jax.random.normal(ks[6], (F_out, D_ff), jnp.float32) * s, 'b1': jnp.zeros((D_ff,), jnp.float32), 'w2': jax.random.normal(ks[7], (D_ff, F_out), jnp.float32) * s, 'b2': jnp.zeros((F_out,), jnp.float32), 'ln_gamma': jnp.ones((F_out,), jnp.float32), 'ln_beta': jnp.zeros((F_out,), jnp.float32)}
    _L1_gnn_all = _L1_gnn_setup()
    _L1_gnn_in = {k: v for k, v in _L1_gnn_all.items() if k in ('W_heads', 'a_heads', 'W_out', 'a_out', 'w1', 'b1', 'w2', 'b2', 'ln_gamma', 'ln_beta')}
    del _L1_gnn_all

    def _L2_gnn_setup():
        import jax, jax.numpy as jnp
        import numpy as np
        B, K, DIN, DOUT = (32, 64, 256, 256)
        key = jax.random.key(seed)
        k1, k2, k3, k4 = jax.random.split(key, 4)
        x = jax.random.normal(k1, (B, K, DIN), dtype=jnp.float32)
        adj = jax.random.randint(k2, (K, K), 0, 2, dtype=jnp.int32)
        W = jax.random.normal(k3, (DOUT, 2 * DIN), dtype=jnp.float32) * 0.02
        b = jax.random.normal(k4, (DOUT,), dtype=jnp.float32) * 0.02
        return {'x': x, 'adj': adj, 'W': W, 'b': b}
    _L2_gnn_all = _L2_gnn_setup()
    _L2_gnn_in = {k: v for k, v in _L2_gnn_all.items() if k in ('W', 'b')}
    del _L2_gnn_all

    def _L3_gnn_setup():
        import jax, jax.numpy as jnp
        import numpy as np
        D_MODEL = 256
        NUM_HEADS = 8
        D_HEAD = D_MODEL // NUM_HEADS
        B, N = (4, 1024)
        key = jax.random.key(seed)
        ks = jax.random.split(key, 10)
        s = 1.0 / np.sqrt(D_MODEL)
        inp = {'h': jax.random.normal(ks[0], (B, N, D_MODEL), dtype=jnp.float32), 'adj': jax.random.randint(ks[1], (N, N), 0, 2, dtype=jnp.int32), 'Wq': jax.random.uniform(ks[2], (D_MODEL, D_MODEL), jnp.float32, -s, s), 'bq': jax.random.uniform(ks[3], (D_MODEL,), jnp.float32, -s, s), 'Wk': jax.random.uniform(ks[4], (D_MODEL, D_MODEL), jnp.float32, -s, s), 'bk': jax.random.uniform(ks[5], (D_MODEL,), jnp.float32, -s, s), 'Wv': jax.random.uniform(ks[6], (D_MODEL, D_MODEL), jnp.float32, -s, s), 'bv': jax.random.uniform(ks[7], (D_MODEL,), jnp.float32, -s, s), 'Wo': jax.random.uniform(ks[8], (D_MODEL, D_MODEL), jnp.float32, -s, s), 'bo': jax.random.uniform(ks[9], (D_MODEL,), jnp.float32, -s, s)}
        return inp
    _L3_gnn_all = _L3_gnn_setup()
    _L3_gnn_in = {k: v for k, v in _L3_gnn_all.items() if k in ('Wq', 'bq', 'Wk', 'bk', 'Wv', 'bv', 'Wo', 'bo')}
    del _L3_gnn_all
    return {'x': x, 'adj': adj, 'L0_gnn_W': _L0_gnn_in['W'], 'L0_gnn_a_src': _L0_gnn_in['a_src'], 'L0_gnn_a_dst': _L0_gnn_in['a_dst'], 'L1_gnn_W_heads': _L1_gnn_in['W_heads'], 'L1_gnn_a_heads': _L1_gnn_in['a_heads'], 'L1_gnn_W_out': _L1_gnn_in['W_out'], 'L1_gnn_a_out': _L1_gnn_in['a_out'], 'L1_gnn_w1': _L1_gnn_in['w1'], 'L1_gnn_b1': _L1_gnn_in['b1'], 'L1_gnn_w2': _L1_gnn_in['w2'], 'L1_gnn_b2': _L1_gnn_in['b2'], 'L1_gnn_ln_gamma': _L1_gnn_in['ln_gamma'], 'L1_gnn_ln_beta': _L1_gnn_in['ln_beta'], 'L2_gnn_W': _L2_gnn_in['W'], 'L2_gnn_b': _L2_gnn_in['b'], 'L3_gnn_Wq': _L3_gnn_in['Wq'], 'L3_gnn_bq': _L3_gnn_in['bq'], 'L3_gnn_Wk': _L3_gnn_in['Wk'], 'L3_gnn_bk': _L3_gnn_in['bk'], 'L3_gnn_Wv': _L3_gnn_in['Wv'], 'L3_gnn_bv': _L3_gnn_in['bv'], 'L3_gnn_Wo': _L3_gnn_in['Wo'], 'L3_gnn_bo': _L3_gnn_in['bo']}

def reference(x, adj, L0_gnn_W, L0_gnn_a_src, L0_gnn_a_dst, L1_gnn_W_heads, L1_gnn_a_heads, L1_gnn_W_out, L1_gnn_a_out, L1_gnn_w1, L1_gnn_b1, L1_gnn_w2, L1_gnn_b2, L1_gnn_ln_gamma, L1_gnn_ln_beta, L2_gnn_W, L2_gnn_b, L3_gnn_Wq, L3_gnn_bq, L3_gnn_Wk, L3_gnn_bk, L3_gnn_Wv, L3_gnn_bv, L3_gnn_Wo, L3_gnn_bo):
    import jax
    import jax.numpy as jnp

    def _L0_gnn_ref(x, adj, W, a_src, a_dst):
        import jax, jax.numpy as jnp
        import numpy as np
        B, N, D = (8, 1024, 256)
        NEG_SLOPE = 0.2
        Wh = jnp.einsum('bnd,de->bne', x, W)
        e_src = jnp.einsum('bnd,d->bn', Wh, a_src)
        e_dst = jnp.einsum('bnd,d->bn', Wh, a_dst)
        logits = e_src[:, :, None] + e_dst[:, None, :]
        logits = jnp.where(logits >= 0, logits, NEG_SLOPE * logits)
        mask = (adj == 0)[None, :, :]
        logits = jnp.where(mask, -jnp.inf, logits)
        attn = jax.nn.softmax(logits, axis=-1)
        attn = jnp.nan_to_num(attn, nan=0.0)
        out = jnp.einsum('bnm,bmd->bnd', attn, Wh)
        return out

    def _L1_gnn_ref(enc_inputs, adj, W_heads, a_heads, W_out, a_out, w1, b1, w2, b2, ln_gamma, ln_beta):
        import jax, jax.numpy as jnp
        import numpy as np
        LEAKY_ALPHA = 0.01
        NEG_INF = -1000000000.0
        LN_EPS = 1e-05

        def _gat_heads(x, adj, W, a):
            O = W.shape[-1]
            Wh = jnp.einsum('bnf,hfo->bhno', x, W)
            f1 = jnp.einsum('bhno,ho->bhn', Wh, a[:, :O])
            f2 = jnp.einsum('bhno,ho->bhn', Wh, a[:, O:])
            e = f1[:, :, :, None] + f2[:, :, None, :]
            e = jnp.where(e > 0, e, LEAKY_ALPHA * e)
            e = jnp.where(adj[None, None] > 0, e, NEG_INF)
            attn = jax.nn.softmax(e, axis=-1)
            return jnp.einsum('bhnm,bhmo->bhno', attn, Wh)
        B, N, _ = enc_inputs.shape
        h = jax.nn.elu(_gat_heads(enc_inputs, adj, W_heads, a_heads))
        h = jnp.transpose(h, (0, 2, 1, 3)).reshape(B, N, -1)
        out = _gat_heads(h, adj, W_out[None], a_out[None])[:, 0]
        out = jax.nn.elu(out)
        ffn = jnp.maximum(out @ w1 + b1, 0.0) @ w2 + b2
        y = ffn + out
        mu = jnp.mean(y, axis=-1, keepdims=True)
        var = jnp.var(y, axis=-1, keepdims=True)
        return (y - mu) / jnp.sqrt(var + LN_EPS) * ln_gamma + ln_beta

    def _L2_gnn_ref(x, adj, W, b):
        import jax, jax.numpy as jnp
        import numpy as np
        B, K, DIN, DOUT = (32, 64, 256, 256)
        Din = x.shape[-1]
        Wi, Wj = (W[:, :Din], W[:, Din:])
        mi = jnp.einsum('bkd,od->bko', x, Wi)
        mj = jnp.einsum('bkd,od->bko', x, Wj)
        a = adj.astype(x.dtype)
        deg = a.sum(axis=1)
        out = deg[None, :, None] * (mi + b) + jnp.einsum('ij,bjo->bio', a, mj)
        return out

    def _L3_gnn_ref(h, adj, Wq, bq, Wk, bk, Wv, bv, Wo, bo):
        import jax, jax.numpy as jnp
        import numpy as np
        D_MODEL = 256
        NUM_HEADS = 8
        D_HEAD = D_MODEL // NUM_HEADS
        B, N = (4, 1024)
        b, n, _ = h.shape

        def split_heads(x):
            return x.reshape(b, n, NUM_HEADS, D_HEAD).transpose(0, 2, 1, 3)
        q = split_heads(h @ Wq.T + bq)
        k = split_heads(h @ Wk.T + bk)
        v = split_heads(h @ Wv.T + bv)
        scale = 1.0 / np.sqrt(D_HEAD)
        scores = jnp.einsum('bhqd,bhkd->bhqk', q, k) * scale
        mask = (adj == 0)[None, None, :, :]
        scores = jnp.where(mask, -jnp.inf, scores)
        attn = jax.nn.softmax(scores, axis=-1)
        out = jnp.einsum('bhqk,bhkd->bhqd', attn, v)
        out = out.transpose(0, 2, 1, 3).reshape(b, n, D_MODEL)
        return out @ Wo.T + bo
    h = jnp.maximum(_layernorm(x, axis=-1), 0.0)
    x = x + _L0_gnn_ref(h, adj, L0_gnn_W, L0_gnn_a_src, L0_gnn_a_dst)
    h = jnp.maximum(_layernorm(x, axis=-1), 0.0)
    x = x + _L1_gnn_ref(h, adj, L1_gnn_W_heads, L1_gnn_a_heads, L1_gnn_W_out, L1_gnn_a_out, L1_gnn_w1, L1_gnn_b1, L1_gnn_w2, L1_gnn_b2, L1_gnn_ln_gamma, L1_gnn_ln_beta)
    h = jnp.maximum(_layernorm(x, axis=-1), 0.0)
    x = x + _L2_gnn_ref(h, adj, L2_gnn_W, L2_gnn_b)
    h = jnp.maximum(_layernorm(x, axis=-1), 0.0)
    x = x + _L3_gnn_ref(h, adj, L3_gnn_Wq, L3_gnn_bq, L3_gnn_Wk, L3_gnn_bk, L3_gnn_Wv, L3_gnn_bv, L3_gnn_Wo, L3_gnn_bo)
    return x

_drawn_inputs = setup_inputs


def setup_inputs(seed=0):
    import zlib

    import numpy as np

    out = dict(_drawn_inputs(seed))
    spreads = {'L1_gnn_b1': (0.0, 0.1),
     'L1_gnn_b2': (0.0, 0.1),
     'L1_gnn_ln_gamma': (1.0, 0.2),
     'L1_gnn_ln_beta': (0.0, 0.1)}
    factors = {'L3_gnn_Wq': 8.0,
     'L3_gnn_bq': 64.0,
     'L3_gnn_Wk': 8.0,
     'L3_gnn_bk': 64.0,
     'L3_gnn_bv': 6.544,
     'L3_gnn_bo': 3.527}
    for name, (base, spread) in spreads.items():
        noise = np.random.default_rng([zlib.crc32(name.encode()), seed]).standard_normal(out[name].shape)
        drawn = base * np.exp(spread * noise) if base else spread * noise
        out[name] = jnp.asarray(drawn.astype(out[name].dtype))
    for name, factor in factors.items():
        out[name] = (out[name] * factor).astype(out[name].dtype)
    return out
```

```python
from contextlib import ExitStack

import concourse.bass as bass
from concourse import mybir

f32 = mybir.dt.float32
f32r = mybir.dt.float32r
i32 = mybir.dt.int32
ALU = mybir.AluOpType
ACT = mybir.ActivationFunctionType
AX = mybir.AxisListType

P = 128
NB, N, D = 32, 256, 256
T = N // P
K = D // P
H1 = 4
H3 = 8
DH = D // H3
SLOTS = 2
ITERS = NB // SLOTS
EPS = 1e-5
MASKED = -1e30
SLOPE = [0.2] + [0.01] * (H1 + 1)
GATS = 2 + H1
ROUNDS = GATS + H3
SCALE = float(DH) ** -0.5
LN0, LN1, LNF, LN2, LN3 = range(5)
NLN = 5
TURN = {LN0: 0, LN1: 1, LN2: 2, LN3: 3}


def slot_steps():
    def norm(n):
        out = [("stats", n), ("coef", n), ("norm", n)]
        return out + ([("turn", n), ("hi", n), ("lo", n)] if n in TURN else [])

    def soften(g):
        return [("dst", g), ("dmax", g), ("leak", g), ("logit", g), ("prob", g)]

    def mix(g):
        return [("pturn", g), ("pvals", g), ("mix", g)]

    def elu(e):
        return [("expo", e), ("elu", e), ("eturn", e), ("eT", e)]

    first = norm(LN0) + [("proj", 0), ("vals", 0), ("sd", 0)] + soften(0) + mix(0) + [("x0", 0)]
    first += norm(LN1)
    for p in range(1, 5):
        first += [("proj", p), ("vals", p)]
    first += [("sdp", 0), ("sd", 1)]
    first += soften(1)
    for h in range(H1):
        if h + 1 < H1:
            a, b = soften(h + 2), mix(h + 1) + elu(h)
            first += [a[0], a[1], b[0], a[2], b[1], a[3], b[2], a[4], *b[3:]]
        else:
            first += mix(h + 1) + elu(h)
    second = [("proj", 5), ("vals", 5), ("sd", 2)] + soften(5) + mix(5) + elu(H1)
    second += [("up", 0), ("relu", 0), ("down", 0), ("ysum", 0)] + norm(LNF) + [("gain", 0), ("x1", 0)]
    second += norm(LN2) + [("msg", 0), ("mhi", 0), ("mlo", 0), ("self", 0), ("nbr", 0), ("x2", 0)]
    second += norm(LN3) + [("q", 0), ("k", 0), ("qs", 0), ("ks", 0), ("v", 0), ("vs", 0)]
    second += [("score", 0), ("smax", 0), ("sprob", 0)]
    for h in range(H3):
        a = [("score", h + 1), ("smax", h + 1), ("sprob", h + 1)] if h + 1 < H3 else []
        b = [("spturn", h), ("spvals", h), ("smix", h), ("onorm", h)]
        second += [x for pair in zip(a + [None], b) for x in pair if x] if a else b
    second += [("oturn", 0), ("oT", 0), ("wo", 0), ("done", 0)]
    return first, second


def merge(lists):
    at = [(( i + 0.5) / len(one), n, i) for n, one in enumerate(lists) for i in range(len(one))]
    return [lists[n][i] for _, n, i in sorted(at)]


def build(nc, x, adj, W0, a0s, a0d, W1, a1, WO1, aO1, w1, b1, w2, b2, gam, bet, W2, b2g,
          Wq, bq, Wk, bk, Wv, bv, Wo, bo, out):
    with ExitStack() as ctx:
        def sb(name, shape, dt=f32):
            return ctx.enter_context(nc.sbuf_tensor(name, [P, *shape], dt))

        def sem(name):
            return ctx.enter_context(nc.semaphore(name))

        def per_slot(name, shape, dt=f32):
            return [sb(f"{name}{s}", shape, dt) for s in range(SLOTS)]

        def sems(name):
            return [sem(f"{name}{s}") for s in range(SLOTS)]

        ident = sb("ident", [P])
        w0h, w0l = sb("w0h", [K, D + 2], f32r), sb("w0l", [K, D + 2], f32r)
        w1h, w1l = sb("w1h", [K, H1 * D], f32r), sb("w1l", [K, H1 * D], f32r)
        a1h, a1l = sb("a1h", [K, 2 * H1], f32r), sb("a1l", [K, 2 * H1], f32r)
        wout = sb("wout", [H1 * K, D + 2])
        wup, wdown = sb("wup", [K, D]), sb("wdown", [K, D])
        w2h, w2l = sb("w2h", [K, 2 * D], f32r), sb("w2l", [K, 2 * D], f32r)
        wqh, wql = sb("wqh", [K, D], f32r), sb("wql", [K, D], f32r)
        wkh, wkl = sb("wkh", [K, D], f32r), sb("wkl", [K, D], f32r)
        wvh, wvl = sb("wvh", [K, D], f32r), sb("wvl", [K, D], f32r)
        woT = sb("woT", [K, D])
        mask = sb("mask", [T, N])
        adjT = sb("adjT", [T, N], f32r)
        deg = sb("deg", [T])
        linked = sb("linked", [T])
        degb = sb("degb", [T, D])
        ffnb = sb("ffnb", [D])
        gamb, betb, bob = sb("gamb", [D]), sb("betb", [D]), sb("bob", [D])
        bcol = sb("bcol", [4 * K])
        b1c, bqc, bkc, bvc = (bcol[:, K * j:K * j + K] for j in range(4))
        minus_half, zero = sb("minus_half", [T]), sb("zero", [T])

        X = per_slot("X", [T, D])
        XB = per_slot("XB", [T, D])
        XO = per_slot("XO", [T, D])
        HN = per_slot("HN", [T, D])
        HH, HL = per_slot("HH", [K, N], f32r), per_slot("HL", [K, N], f32r)
        ST, MV = per_slot("ST", [T, 6]), per_slot("MV", [T, 2])
        VE, NM, RS, NMR = (per_slot(n, [T]) for n in ("VE", "NM", "RS", "NMR"))
        VAL = per_slot("VAL", [T, H1 * D])
        SD = per_slot("SD", [T, 2 * H1])
        NAS = per_slot("NAS", [T, H1])
        SMX = [per_slot(f"SMX{j}_", [T]) for j in range(2)]
        NDM, U, NMX = per_slot("NDM", [T]), per_slot("U", [T]), per_slot("NMX", [T])
        LG = [per_slot(f"LG{j}_", [T, N]) for j in range(2)]
        LK = per_slot("LK", [T, N])
        PR = [per_slot(f"PR{j}_", [T, N]) for j in range(2)]
        SUM = [per_slot(f"SUM{j}_", [T]) for j in range(2)]
        RI = [per_slot(f"RI{j}_", [T]) for j in range(2)]
        PT = per_slot("PT", [T, N])
        EX, PO, EL = per_slot("EX", [T, D]), per_slot("PO", [T, D]), per_slot("EL", [T, D])
        ET = per_slot("ET", [H1 * K, N])
        OT = per_slot("OT", [K, N])
        F1 = per_slot("F1", [K, N])
        Y = per_slot("Y", [T, D])
        MH, ML = per_slot("MH", [T, D], f32r), per_slot("ML", [T, D], f32r)
        QT = [v[:, :, 0:N] for v in VAL]
        KT = [v[:, :, N:2 * N] for v in VAL]
        VV = [v[:, :, 2 * N:3 * N] for v in VAL]
        O3 = [v[:, :, 3 * N:4 * N] for v in VAL]

        def banks(name):
            return [ctx.enter_context(nc.psum_tensor(f"{name}{s}", [P, 512], f32)) for s in range(SLOTS)]
        turnb, probb, mm0, mm1 = banks("turnb"), banks("probb"), banks("mm0"), banks("mm1")
        mmb = [[mm0[s], mm1[s]] for s in range(SLOTS)]

        def two(ap):
            return ap[:, :].rearrange("p (t n) -> p t n", t=2)

        w_in = [sem(f"w_in{j}") for j in range(4)]
        set_dve, set_pool, set_pe = sem("set_dve"), sem("set_pool"), sem("set_pe")
        reducing = sem("reducing")
        x_in, stored = sems("x_in"), sems("stored")
        stats, coef_up, normed = sems("stats"), sems("coef_up"), sems("normed")
        turned, hi_up, lo_up = sems("turned"), sems("hi_up"), sems("lo_up")
        proj_up, vals_up, sdp_up, sd_up = sems("proj_up"), sems("vals_up"), sems("sdp_up"), sems("sd_up")
        dst_up, dmax_up, nmx_up, leak_up, logit_up = (sems(n) for n in
                                                      ("dst_up", "dmax_up", "nmx_up", "leak_up", "logit_up"))
        prob_up, pturned, pvals_up, mixed = sems("prob_up"), sems("pturned"), sems("pvals_up"), sems("mixed")
        rinv_up = sems("rinv_up")
        expo_up, elu_up, eturned, eT_up = sems("expo_up"), sems("elu_up"), sems("eturned"), sems("eT_up")
        x_up, xb_up = sems("x_up"), sems("xb_up")
        up_up, relu_up, down_up, gb_up, gain_up = (sems(n) for n in
                                                   ("up_up", "relu_up", "down_up", "gb_up", "gain_up"))
        msg_up, mhi_up, mlo_up, self_up, nbr_up = (sems(n) for n in
                                                   ("msg_up", "mhi_up", "mlo_up", "self_up", "nbr_up"))
        qkv_up, qs_up, ks_up, vs_up = sems("qkv_up"), sems("qs_up"), sems("ks_up"), sems("vs_up")
        score_up, smax_up, o_up = sems("score_up"), sems("smax_up"), sems("o_up")
        oturned, oT_up, wo_up, done = sems("oturned"), sems("oT_up"), sems("wo_up"), sems("done")

        first, second = slot_steps()
        GA, GB = list(range(SLOTS // 2)), list(range(SLOTS // 2, SLOTS))

        def tag(steps, group, late):
            return [[(name, s, late, arg) for name, arg in steps] for s in group]

        def walk(eng, handlers):
            def run(steps, it):
                for name, s, late, arg in steps:
                    if name in handlers:
                        handlers[name](s, it + late if late else it, arg)
            run(merge(tag(first, GA, 0)), 0)
            with eng.Fori(0, ITERS - 1) as it:
                run(merge(tag(second, GA, 0) + tag(first, GB, 0)), it)
                run(merge(tag(first, GA, 1) + tag(second, GB, 0)), it)
            run(merge(tag(second, GA, 0) + tag(first, GB, 0)), ITERS - 1)
            run(merge(tag(second, GB, 0)), ITERS - 1)

        def wait(eng, s_, it, per_pass, n):
            eng.wait_ge(s_, it * per_pass + n)

        raw = {n: ET[0][:, 2 * j:2 * j + 2, :] for j, n in enumerate(("Wq", "Wk", "Wv", "Wo"))}
        raw2 = VAL[0][:, 0:2, 0:2 * D]
        raw0 = VAL[0][:, :, 2 * D:3 * D]
        raw1 = VAL[1][:, :, :]
        adji = PR[0][0][:, :, :].bitcast(i32)
        adjf = PR[1][0]
        av = ET[1]
        junk = LK[0]
        brow = LK[1][:, 0, 0:P]
        a0b = PO[0]
        aOb = PO[1]

        WA, WA1 = sb("WA", [K, 2]), sb("WA1", [K, 2 * H1])
        whole = slice(0, D)
        TURNS = [(adjT, None, whole), (wqh, wql, whole), (wkh, wkl, whole), (wvh, wvl, whole),
                 (w2h, w2l, slice(0, D)), (w2h, w2l, slice(D, 2 * D)), (woT, None, whole)]
        TURN_SRC = [adjf[:, :, :], raw["Wq"], raw["Wk"], raw["Wv"], raw2[:, :, 0:D], raw2[:, :, D:2 * D], raw["Wo"]]
        TURN_MARKS = [17, 19, 21, 23, 25, 27, 28]
        SET_ALL = 29
        turn_marks = []
        w_counts = []

        with nc.Block() as block:
            @block.sync
            def _(sp):
                def bc(v):
                    return v.partition_broadcast(P)
                g0 = [(adji, adj.rearrange("(t p) n -> p t n", p=P)),
                      (wup[:, :, :], w1.rearrange("(t p) n -> p t n", p=P)),
                      (wdown[:, :, :], w2.rearrange("(t p) n -> p t n", p=P)),
                      (wout[:, :, 0:D], WO1.rearrange("(t p) n -> p t n", p=P))]
                g1 = [(raw0, W0.rearrange("(t p) n -> p t n", p=P)),
                      (a0b[:, 0, :], bc(a0s)), (a0b[:, 1, :], bc(a0d)),
                      (aOb[:, 0, :], bc(aO1[0:D])), (aOb[:, 1, :], bc(aO1[D:2 * D]))]
                g1 += [(raw1[:, :, h * D:(h + 1) * D], W1[h].rearrange("(t p) n -> p t n", p=P)) for h in range(H1)]
                g1 += [(av[:, 2 * h + j, :], bc(a1[h, j * D:(j + 1) * D])) for h in range(H1) for j in range(2)]
                g2 = [(raw[n], w.rearrange("(t p) n -> p t n", p=P))
                      for n, w in (("Wq", Wq), ("Wk", Wk), ("Wv", Wv), ("Wo", Wo))]
                g2 += [(raw2, W2.rearrange("(t p) n -> p t n", p=P))]
                g3 = [(degb[:, 0, :], bc(b2g)), (degb[:, 1, :], bc(b2g)), (ffnb[:, :], bc(b2)),
                      (gamb[:, :], bc(gam)), (betb[:, :], bc(bet)), (bob[:, :], bc(bo))]
                g3 += [(brow[2 * j:2 * j + 2, :], v.rearrange("(t p) -> t p", p=P)) for j, v in enumerate((b1, bq, bk, bv))]
                for j, g in enumerate((g0, g1, g2, g3)):
                    for dst, src in g:
                        sp.dma_start(dst, src).then_inc(w_in[j], 16)
                w_counts.extend(16 * len(g) for g in (g0, g1, g2, g3))

                def rows(dram, it, s):
                    return dram[bass.ds(it * SLOTS + s, 1), :, :].rearrange("a (t p) d -> p (a t) d", p=P)

                for s in range(SLOTS):
                    sp.dma_start(X[s][:, :, :], rows(x, 0, s)).then_inc(x_in[s], 16)
                with sp.Fori(0, ITERS - 1) as it:
                    for s in range(SLOTS):
                        wait(sp, xb_up[s], it, 3, 3)
                        wait(sp, normed[s], it, NLN, NLN)
                        sp.dma_start(X[s][:, :, :], rows(x, it + 1, s)).then_inc(x_in[s], 16)
                        wait(sp, done[s], it, 1, 1)
                        sp.dma_start(rows(out, it, s), XO[s][:, :, :]).then_inc(stored[s], 16)
                for s in range(SLOTS):
                    wait(sp, done[s], ITERS - 1, 1, 1)
                    sp.dma_start(rows(out, ITERS - 1, s), XO[s][:, :, :]).then_inc(stored[s], 16)
                for s in range(SLOTS):
                    sp.wait_ge(stored[s], 16 * ITERS + 1)

            @block.gpsimd
            def _(pool):
                pool.memset(ident[:, :], 0.0).then_inc(set_pool, 1)
                pool.memset(minus_half[:, :], -0.5).then_inc(set_pool, 1)
                pool.memset(zero[:, :], 0.0).then_inc(set_pool, 1)
                pool.wait_ge(set_pool, 3)
                pool.affine_select(out=ident[:, :], in_=ident[:, :], compare_op=ALU.not_equal, fill=1.0,
                                   base=0, pattern=[[-1, P]], channel_multiplier=1).then_inc(set_pool, 1)
                pool.wait_ge(set_dve, SET_ALL)

                def coef(s, it, n):
                    wait(pool, stats[s], it, NLN, n + 1)
                    pool.tensor_tensor(NM[s][:, :], zero[:, :], MV[s][:, :, 0], ALU.subtract)
                    pool.tensor_scalar(VE[s][:, :], MV[s][:, :, 1], EPS, 1.0, ALU.add, ALU.mult)
                    pool.drain()
                    pool.tensor_tensor(RS[s][:, :], VE[s][:, :], minus_half[:, :], ALU.pow)
                    pool.drain()
                    pool.tensor_tensor(NMR[s][:, :], NM[s][:, :], RS[s][:, :], ALU.mult).then_inc(coef_up[s], 1)
                    if n == LN1:
                        add_bias(s, it, 0)
                    if n == LN2:
                        add_bias(s, it, 1)
                    if n == LN3:
                        add_bias(s, it, 2)

                def add_bias(s, it, j):
                    for t in range(T):
                        b = (betb[:, :], degb[:, t, :], bob[:, :])[j]
                        ins = pool.tensor_tensor(XB[s][:, t, :], X[s][:, t, :], b, ALU.add)
                    ins.then_inc(xb_up[s], 1)

                def gb(s, it, _):
                    wait(pool, eT_up[s], it, H1 + 1, H1 + 1)
                    for t in range(T):
                        ins = pool.tensor_tensor(EL[s][:, t, :], EL[s][:, t, :], ffnb[:, :], ALU.add)
                    ins.then_inc(gb_up[s], 1)

                def gain(s, it, _):
                    wait(pool, normed[s], it, NLN, LNF + 1)
                    for t in range(T):
                        ins = pool.tensor_tensor(Y[s][:, t, :], HN[s][:, t, :], gamb[:, :], ALU.mult)
                    ins.then_inc(gain_up[s], 1)

                walk(pool, {"coef": coef, "up": gb, "gain": gain})

            @block.scalar
            def _(act):
                act.wait_ge(set_dve, SET_ALL)

                def norm(s, it, n):
                    wait(act, coef_up[s], it, NLN, n + 1)
                    f = ACT.Identity if n == LNF else ACT.Relu
                    src = Y if n == LNF else X
                    for t in range(T):
                        ins = act.activation(HN[s][:, t, :], src[s][:, t, :], f, bias=NMR[s][:, t:t + 1],
                                             scale=RS[s][:, t:t + 1])
                    ins.then_inc(normed[s], 1)

                def hi(s, it, n):
                    wait(act, turned[s], it, 4, TURN[n] + 1)
                    act.activation(HH[s][:, :, :], two(turnb[s]), ACT.Copy).then_inc(hi_up[s], 1)

                def vals(s, it, p):
                    wait(act, proj_up[s], it, 6, p + 1)
                    if p in (0, 5):
                        for t in range(T):
                            ins = act.activation(VAL[s][:, t, 0:D], mmb[s][t][:, 0:D], ACT.Copy)
                    else:
                        t, c = (p - 1) // 2, (p - 1) % 2
                        ins = act.activation(VAL[s][:, t, c * 512:(c + 1) * 512], mmb[s][(p - 1) % 2][:, :], ACT.Copy)
                    ins.then_inc(vals_up[s], 1)

                def leak(s, it, g):
                    wait(act, dmax_up[s], it, GATS, g + 1)
                    h = g - 1 if 1 <= g <= H1 else 0
                    for t in range(T):
                        ins = act.activation(LK[s][:, t, :], LG[0][s][:, t, :], ACT.Identity,
                                             bias=NAS[s][:, t, h:h + 1], scale=SLOPE[g])
                    ins.then_inc(leak_up[s], 1)

                def prob(s, it, g):
                    wait(act, logit_up[s], it, GATS, g + 1)
                    for t in range(T):
                        ins = act.activation(PR[g % 2][s][:, t, :], LG[0][s][:, t, :], ACT.Exp,
                                             bias=NMX[s][:, t:t + 1], scale=-1.0, accum_out=SUM[g % 2][s][:, t:t + 1])
                    ins.then_inc(prob_up[s], 1)

                def sprob(s, it, h):
                    wait(act, smax_up[s], it, H3, h + 1)
                    r = GATS + h
                    for t in range(T):
                        ins = act.activation(PR[r % 2][s][:, t, :], LG[h % 2][s][:, t, :], ACT.Exp,
                                             bias=SMX[h % 2][s][:, t:t + 1], scale=-1.0,
                                             accum_out=SUM[r % 2][s][:, t:t + 1])
                    ins.then_inc(prob_up[s], 1)

                def pvals(s, it, r):
                    wait(act, pturned[s], it, ROUNDS, r + 1)
                    act.activation(PT[s][:, :, :], two(probb[s]), ACT.Copy).then_inc(pvals_up[s], 1)

                def expo(s, it, e):
                    wait(act, rinv_up[s], it, ROUNDS, e + 2)
                    wait(act, mixed[s], it, ROUNDS, e + 2)
                    g = e + 1
                    for t in range(T):
                        ins = act.activation(EX[s][:, t, :], mmb[s][g % 2][:, t * D:(t + 1) * D], ACT.Exp,
                                             scale=RI[g % 2][s][:, t:t + 1])
                    ins.then_inc(expo_up[s], 1)

                def relu(s, it, _):
                    wait(act, up_up[s], it, 1, 1)
                    for t in range(K):
                        ins = act.activation(F1[s][:, t, :], mm0[s][:, t * N:(t + 1) * N], ACT.Relu, bias=b1c[:, t:t + 1])
                    ins.then_inc(relu_up[s], 1)

                def mhi(s, it, _):
                    wait(act, msg_up[s], it, 1, 1)
                    for t in range(T):
                        ins = act.activation(MH[s][:, t, :], mmb[s][t][:, D:2 * D], ACT.Copy)
                    ins.then_inc(mhi_up[s], 1)

                def qs(s, it, _):
                    wait(act, qkv_up[s], it, 3, 1)
                    for t in range(K):
                        ins = act.activation(QT[s][:, t, :], mm0[s][:, t * N:(t + 1) * N], ACT.Identity, bias=bqc[:, t:t + 1])
                    ins.then_inc(qs_up[s], 1)

                def vs(s, it, _):
                    wait(act, qkv_up[s], it, 3, 3)
                    act.activation(VV[s], two(probb[s]), ACT.Copy).then_inc(vs_up[s], 1)

                def oT(s, it, _):
                    wait(act, oturned[s], it, 1, 1)
                    act.activation(OT[s][:, :, :], two(probb[s]), ACT.Copy).then_inc(oT_up[s], 1)

                walk(act, {"norm": norm, "hi": hi, "vals": vals, "leak": leak, "prob": prob, "sprob": sprob,
                           "pvals": pvals, "spvals": lambda s, it, h: pvals(s, it, GATS + h), "expo": expo,
                           "relu": relu, "mhi": mhi, "qs": qs, "vs": vs, "oT": oT})

            @block.vector
            def _(dve):
                count = [0]

                def mark(ins):
                    count[0] += 1
                    ins.then_inc(set_dve, 1)

                def split(hi, lo, src):
                    mark(dve.tensor_copy(hi, src))
                    dve.wait_ge(set_dve, count[0])
                    mark(dve.tensor_tensor(lo, src, hi.bitcast(f32), ALU.subtract))

                dve.wait_ge(w_in[0], w_counts[0])
                mark(dve.tensor_copy(adjf[:, :, :], adji))
                dve.wait_ge(set_dve, count[0])
                mark(dve.tensor_scalar(mask[:, :, :], adjf[:, :, :], 0.0, MASKED, ALU.is_equal, ALU.mult))
                mark(dve.tensor_reduce(deg[:, :], adjf[:, :, :], AX.X, ALU.add))
                dve.wait_ge(set_dve, count[0])
                mark(dve.tensor_reduce(linked[:, :], adjf[:, :, :], AX.X, ALU.max))
                dve.wait_ge(w_in[3], w_counts[3])
                for t in range(T):
                    mark(dve.tensor_scalar(degb[:, t, :], degb[:, t, :], deg[:, t:t + 1], None, ALU.mult))
                mark(dve.tensor_scalar(ffnb[:, :], ffnb[:, :], -1.0, None, ALU.add))

                def dot(dst, rows, vec):
                    dve.tensor_tensor_reduce(out=junk[:, 0, :], in0=rows, in1=vec, scale=1.0, scalar=0.0,
                                             op0=ALU.mult, op1=ALU.add, accum_out=dst)
                    dve.drain()

                dve.wait_ge(w_in[1], w_counts[1])
                for t in range(K):
                    for j in range(2):
                        dot(WA[:, t, j:j + 1], raw0[:, t, :], a0b[:, j, :])
                        for h in range(H1):
                            dot(WA1[:, t, j * H1 + h:j * H1 + h + 1], raw1[:, t, h * D:(h + 1) * D], av[:, 2 * h + j, :])
                for t in range(H1 * K):
                    for j in range(2):
                        dot(wout[:, t, D + j:D + j + 1], wout[:, t, 0:D], aOb[:, j, :])
                split(w0h[:, :, 0:D], w0l[:, :, 0:D], raw0)
                split(w0h[:, :, D:D + 2], w0l[:, :, D:D + 2], WA[:, :, :])
                split(w1h[:, :, :], w1l[:, :, :], raw1)
                split(a1h[:, :, :], a1l[:, :, :], WA1[:, :, :])

                dve.wait_ge(set_pe, 1)
                mark(dve.tensor_copy(bcol[:, :], probb[0][:, 0:4 * K]))
                n = 0
                for hi, lo, cols in TURNS:
                    n += 1
                    src = two(turnb[n % 2])
                    dve.wait_ge(set_pe, n + 1)
                    if hi is woT:
                        mark(dve.tensor_copy(woT[:, :, :], src))
                    elif hi is adjT:
                        mark(dve.tensor_copy(adjT[:, :, :], src))
                    else:
                        split(hi[:, :, cols], lo[:, :, cols], src)
                    turn_marks.append(count[0])
                dve.wait_ge(set_pe, n + 2)
                mark(dve.tensor_tensor(bob[:, :], mm0[0][:, 0:D], bob[:, :], ALU.add))
                assert count[0] == SET_ALL, count
                assert turn_marks == TURN_MARKS, turn_marks

                def stats_(s, it, n):
                    if n == LN0:
                        wait(dve, x_in[s], it, 16, 16)
                    src = Y if n == LNF else X
                    for t in range(T):
                        dve.bn_stats(ST[s][:, t, :], src[s][:, t, :])
                    dve.drain()
                    for t in range(T):
                        ins = dve.bn_aggr(MV[s][:, t, :], ST[s][:, t, :])
                    ins.then_inc(stats[s], 1)

                def lo(s, it, n):
                    wait(dve, hi_up[s], it, 4, TURN[n] + 1)
                    dve.tensor_tensor(HL[s][:, :, :], two(turnb[s]), HH[s][:, :, :].bitcast(f32),
                                      ALU.subtract).then_inc(lo_up[s], 1)

                def sd(s, it, l):
                    heads = H1 if l == 1 else 1
                    if l == 1:
                        wait(dve, sdp_up[s], it, 1, 1)
                        dve.tensor_copy(SD[s][:, :, :], turnb[s][:, 0:4 * H1].rearrange("p (t n) -> p t n", t=T))
                    else:
                        wait(dve, vals_up[s], it, 6, 6 if l else 1)
                        for t in range(T):
                            dve.tensor_copy(SD[s][:, t, 0:2], mmb[s][t][:, D:D + 2])
                    dve.drain()
                    dve.tensor_scalar(NAS[s][:, :, 0:heads], SD[s][:, :, 0:heads], -SLOPE[l], None,
                                      ALU.mult).then_inc(sd_up[s], 1)

                def dmax(s, it, g):
                    wait(dve, dst_up[s], it, GATS, g + 1)
                    if g:
                        wait(dve, prob_up[s], it, ROUNDS, g)
                    h = g - 1 if 1 <= g <= H1 else 0
                    dve.sem_inc(reducing, 1)
                    for t in range(T):
                        ins = dve.tensor_tensor_reduce(out=LG[0][s][:, t, :], in0=turnb[s][:, 0:N], in1=mask[:, t, :],
                                                       scale=-1.0, scalar=3.0e38, op0=ALU.add, op1=ALU.min,
                                                       accum_out=NDM[s][:, t:t + 1])
                    ins.then_inc(dmax_up[s], 1)
                    dve.drain()
                    dve.tensor_tensor(U[s][:, :], NDM[s][:, :], SD[s][:, :, h], ALU.subtract)
                    dve.drain()
                    dve.scalar_tensor_tensor(NMX[s][:, :], U[s][:, :], SLOPE[g], U[s][:, :], ALU.mult, ALU.min)

                def logit(s, it, g):
                    wait(dve, leak_up[s], it, GATS, g + 1)
                    h = g - 1 if 1 <= g <= H1 else 0
                    for t in range(T):
                        ins = dve.scalar_tensor_tensor(LG[0][s][:, t, :], LG[0][s][:, t, :], SD[s][:, t, h:h + 1],
                                                       LK[s][:, t, :], ALU.subtract, ALU.min)
                    ins.then_inc(logit_up[s], 1)

                def rinv(s, it, r):
                    wait(dve, prob_up[s], it, ROUNDS, r + 1)
                    ins = dve.reciprocal(RI[r % 2][s][:, :], SUM[r % 2][s][:, :])
                    if r == 0:
                        dve.drain()
                        ins = dve.tensor_tensor(RI[0][s][:, :], RI[0][s][:, :], linked[:, :], ALU.mult)
                    ins.then_inc(rinv_up[s], 1)

                def x0(s, it, _):
                    dve.drain()
                    wait(dve, mixed[s], it, ROUNDS, 1)
                    for t in range(T):
                        ins = dve.scalar_tensor_tensor(X[s][:, t, :], mm0[s][:, t * D:(t + 1) * D], RI[0][s][:, t:t + 1],
                                                       X[s][:, t, :], ALU.mult, ALU.add)
                    ins.then_inc(x_up[s], 1)
                    dve.drain()

                def elu(s, it, e):
                    g = e + 1
                    if e:
                        wait(dve, eturned[s], it, H1 + 1, e)
                    wait(dve, expo_up[s], it, H1 + 1, e + 1)
                    for t in range(T):
                        dve.tensor_scalar(PO[s][:, t, :], mmb[s][g % 2][:, t * D:(t + 1) * D], RI[g % 2][s][:, t:t + 1],
                                          0.0, ALU.mult, ALU.max)
                    dve.drain()
                    dve.scalar_tensor_tensor(EL[s][:, :, :], EX[s][:, :, :], 1.0, PO[s][:, :, :], ALU.min,
                                             ALU.add).then_inc(elu_up[s], 1)

                def eT(s, it, e):
                    wait(dve, eturned[s], it, H1 + 1, e + 1)
                    dst = OT[s][:, :, :] if e == H1 else ET[s][:, 2 * e:2 * e + 2, :]
                    dve.tensor_scalar(dst, two(turnb[s]), -1.0, None, ALU.add).then_inc(eT_up[s], 1)

                def ysum(s, it, _):
                    wait(dve, gb_up[s], it, 1, 1)
                    wait(dve, down_up[s], it, 1, 1)
                    dve.tensor_tensor(Y[s][:, :, :], two(mm1[s]), EL[s][:, :, :], ALU.add)
                    dve.drain()

                def x1(s, it, _):
                    wait(dve, xb_up[s], it, 3, 1)
                    wait(dve, gain_up[s], it, 1, 1)
                    dve.tensor_tensor(X[s][:, :, :], Y[s][:, :, :], XB[s][:, :, :], ALU.add).then_inc(x_up[s], 1)
                    dve.drain()

                def mlo(s, it, _):
                    wait(dve, mhi_up[s], it, 1, 1)
                    for t in range(T):
                        ins = dve.tensor_tensor(ML[s][:, t, :], mmb[s][t][:, D:2 * D], MH[s][:, t, :].bitcast(f32),
                                                ALU.subtract)
                    ins.then_inc(mlo_up[s], 1)

                def own(s, it, _):
                    wait(dve, xb_up[s], it, 3, 2)
                    for t in range(T):
                        ins = dve.scalar_tensor_tensor(X[s][:, t, :], mmb[s][t][:, 0:D], deg[:, t:t + 1],
                                                       XB[s][:, t, :], ALU.mult, ALU.add)
                    ins.then_inc(self_up[s], 1)
                    dve.drain()

                def x2(s, it, _):
                    wait(dve, nbr_up[s], it, 1, 1)
                    dve.tensor_tensor(X[s][:, :, :], two(probb[s]), X[s][:, :, :], ALU.add).then_inc(x_up[s], 1)
                    dve.drain()

                def ks(s, it, _):
                    wait(dve, qkv_up[s], it, 3, 2)
                    for t in range(K):
                        ins = dve.tensor_scalar(KT[s][:, t, :], mm1[s][:, t * N:(t + 1) * N], bkc[:, t:t + 1], None, ALU.add)
                    ins.then_inc(ks_up[s], 1)

                def smax(s, it, h):
                    wait(dve, score_up[s], it, H3, h + 1)
                    if h >= 2:
                        wait(dve, prob_up[s], it, ROUNDS, GATS + h - 1)
                    dve.sem_inc(reducing, 1)
                    for t in range(T):
                        ins = dve.tensor_tensor_reduce(out=LG[h % 2][s][:, t, :], in0=mmb[s][h % 2][:, t * N:(t + 1) * N],
                                                       in1=mask[:, t, :], scale=-SCALE, scalar=3.0e38, op0=ALU.add,
                                                       op1=ALU.min, accum_out=SMX[h % 2][s][:, t:t + 1])
                    ins.then_inc(smax_up[s], 1)

                def onorm(s, it, h):
                    r = GATS + h
                    rinv(s, it, r)
                    dve.drain()
                    wait(dve, mixed[s], it, ROUNDS, r + 1)
                    for t in range(T):
                        ins = dve.tensor_scalar(O3[s][:, t, h * DH:(h + 1) * DH], turnb[s][:, t * DH:(t + 1) * DH],
                                                RI[r % 2][s][:, t:t + 1], None, ALU.mult)
                    ins.then_inc(o_up[s], 1)

                def finish(s, it, _):
                    wait(dve, xb_up[s], it, 3, 3)
                    dve.wait_ge(stored[s], it * 16 + 1)
                    wait(dve, wo_up[s], it, 1, 1)
                    dve.tensor_tensor(XO[s][:, :, :], two(mm0[s]), XB[s][:, :, :], ALU.add).then_inc(done[s], 1)

                for s in range(SLOTS):
                    dve.sem_inc(stored[s], 1)
                walk(dve, {"stats": stats_, "lo": lo, "sd": sd, "dmax": dmax, "logit": logit, "pvals": rinv, "x0": x0,
                           "elu": elu, "eT": eT, "ysum": ysum, "x1": x1, "mlo": mlo, "self": own, "x2": x2,
                           "ks": ks, "smax": smax, "onorm": onorm, "done": finish})

            @block.tensor
            def _(pe):
                pe.wait_ge(set_pool, 4)
                pe.wait_ge(w_in[2], w_counts[2])
                pe.wait_ge(set_dve, 1)
                pe.wait_ge(w_in[3], w_counts[3])
                pe.transpose(probb[0][:, 0:4 * K], brow[0:4 * K, :], ident[0:4 * K, 0:4 * K]).then_inc(set_pe, 1)
                n = 0
                for hi, lo, cols in TURNS:
                    n += 1
                    if n > 2:
                        pe.wait_ge(set_dve, TURN_MARKS[n - 3])
                    for k in range(K):
                        for t in range(2):
                            src = TURN_SRC[n - 1][:, t, k * P:(k + 1) * P]
                            last = pe.transpose(turnb[n % 2][:, k * 256 + t * P:k * 256 + (t + 1) * P], src, ident[:, :])
                    last.then_inc(set_pe, 1)
                pe.wait_ge(set_dve, SET_ALL - 1)
                pe.wait_ge(w_in[3], w_counts[3])
                for k in range(K):
                    last = pe.matmul(mm0[0][:, 0:D], bvc[:, k:k + 1].to_broadcast([P, P]), woT[:, k, :],
                                     start=(k == 0), stop=(k == K - 1))
                last.then_inc(set_pe, 1)
                pe.wait_ge(set_dve, SET_ALL)

                def three(bank, stat, mov):
                    ops = [(k, a, b) for k in range(K) for a, b in ((0, 0), (0, 1), (1, 0))]
                    for n, (k, a, b) in enumerate(ops):
                        last = pe.matmul(bank, stat(a, k), mov(b, k), start=(n == 0), stop=(n == len(ops) - 1))
                    return last

                def turn(s, it, n):
                    wait(pe, normed[s], it, NLN, n + 1)
                    for k in range(K):
                        for t in range(T):
                            last = pe.transpose(turnb[s][:, k * N + t * P:k * N + (t + 1) * P],
                                                HN[s][:, t, k * P:(k + 1) * P], ident[:, :])
                    last.then_inc(turned[s], 1)

                def h_tile(s, t):
                    return lambda a, k: (HH, HL)[a][s][:, k, t * P:(t + 1) * P]

                def h_all(s):
                    return lambda a, k: (HH, HL)[a][s][:, k, :]

                def proj(s, it, p):
                    if p == 0:
                        wait(pe, lo_up[s], it, 4, 1)
                        for t in range(T):
                            last = three(mmb[s][t][:, 0:D + 2], h_tile(s, t), lambda b, k: (w0h, w0l)[b][:, k, :])
                    elif p == 5:
                        wait(pe, eT_up[s], it, H1 + 1, H1)
                        for t in range(T):
                            for k in range(H1 * K):
                                last = pe.matmul(mmb[s][t][:, 0:D + 2], ET[s][:, k, t * P:(t + 1) * P], wout[:, k, :],
                                                 start=(k == 0), stop=(k == H1 * K - 1))
                    else:
                        if p == 1:
                            wait(pe, lo_up[s], it, 4, 2)
                        if p > 2:
                            wait(pe, vals_up[s], it, 6, p - 1)
                        t, c = (p - 1) // 2, (p - 1) % 2
                        last = three(mmb[s][(p - 1) % 2][:, :], h_tile(s, t),
                                     lambda b, k: (w1h, w1l)[b][:, k, c * 512:(c + 1) * 512])
                    last.then_inc(proj_up[s], 1)

                def sdp(s, it, _):
                    for t in range(T):
                        last = three(turnb[s][:, t * 2 * H1:(t + 1) * 2 * H1], h_tile(s, t),
                                     lambda b, k: (a1h, a1l)[b][:, k, :])
                    last.then_inc(sdp_up[s], 1)

                def dst(s, it, g):
                    wait(pe, sd_up[s], it, 3, 1 if g == 0 else 3 if g == 5 else 2)
                    if 2 <= g <= H1:
                        wait(pe, dmax_up[s], it, GATS, g)
                    if 3 <= g <= H1:
                        wait(pe, eT_up[s], it, H1 + 1, g - 2)
                    c = H1 + g - 1 if 1 <= g <= H1 else 1
                    for t in range(T):
                        last = pe.transpose(turnb[s][:, t * P:(t + 1) * P], SD[s][:, t, c:c + 1].to_broadcast([P, P]),
                                            ident[:, :])
                    last.then_inc(dst_up[s], 1)

                def pturn(s, it, r):
                    wait(pe, prob_up[s], it, ROUNDS, r + 1)
                    if r:
                        wait(pe, pvals_up[s], it, ROUNDS, r)
                    for j in range(T):
                        for t in range(T):
                            last = pe.transpose(probb[s][:, j * N + t * P:j * N + (t + 1) * P],
                                                PR[r % 2][s][:, t, j * P:(j + 1) * P], ident[:, :])
                    last.then_inc(pturned[s], 1)

                def mix(s, it, g):
                    wait(pe, pvals_up[s], it, ROUNDS, g + 1)
                    if g >= 3 and g <= H1:
                        wait(pe, elu_up[s], it, H1 + 1, g - 2)
                    h = g - 1 if 1 <= g <= H1 else 0
                    for t in range(T):
                        for j in range(T):
                            last = pe.matmul(mmb[s][g % 2][:, t * D:(t + 1) * D], PT[s][:, j, t * P:(t + 1) * P],
                                             VAL[s][:, j, h * D:(h + 1) * D], start=(j == 0), stop=(j == T - 1))
                    last.then_inc(mixed[s], 1)

                def eturn(s, it, e):
                    wait(pe, elu_up[s], it, H1 + 1, e + 1)
                    if e + 2 <= H1:
                        wait(pe, dmax_up[s], it, GATS, e + 3)
                    for k in range(K):
                        for t in range(T):
                            last = pe.transpose(turnb[s][:, k * N + t * P:k * N + (t + 1) * P],
                                                EL[s][:, t, k * P:(k + 1) * P], ident[:, :])
                    last.then_inc(eturned[s], 1)

                def up(s, it, _):
                    wait(pe, eT_up[s], it, H1 + 1, H1 + 1)
                    for t in range(K):
                        for k in range(K):
                            last = pe.matmul(mm0[s][:, t * N:(t + 1) * N], wup[:, k, t * P:(t + 1) * P], OT[s][:, k, :],
                                             start=(k == 0), stop=(k == K - 1))
                    last.then_inc(up_up[s], 1)

                def down(s, it, _):
                    wait(pe, relu_up[s], it, 1, 1)
                    for t in range(T):
                        for k in range(K):
                            last = pe.matmul(mm1[s][:, t * D:(t + 1) * D], F1[s][:, k, t * P:(t + 1) * P], wdown[:, k, :],
                                             start=(k == 0), stop=(k == K - 1))
                    last.then_inc(down_up[s], 1)

                def msg(s, it, _):
                    wait(pe, lo_up[s], it, 4, 3)
                    for t in range(T):
                        last = three(mmb[s][t][:, :], h_tile(s, t), lambda b, k: (w2h, w2l)[b][:, k, :])
                    last.then_inc(msg_up[s], 1)

                def nbr(s, it, _):
                    wait(pe, mlo_up[s], it, 1, 1)
                    for t in range(T):
                        ops = [(j, m) for j in range(T) for m in (MH, ML)]
                        for n, (j, m) in enumerate(ops):
                            last = pe.matmul(probb[s][:, t * D:(t + 1) * D], adjT[:, j, t * P:(t + 1) * P], m[s][:, j, :],
                                             start=(n == 0), stop=(n == len(ops) - 1))
                    last.then_inc(nbr_up[s], 1)

                def q(s, it, _):
                    wait(pe, lo_up[s], it, 4, 4)
                    for t in range(K):
                        last = three(mm0[s][:, t * N:(t + 1) * N],
                                     lambda a, k: (wqh, wql)[a][:, k, t * P:(t + 1) * P], h_all(s))
                    last.then_inc(qkv_up[s], 1)

                def k_(s, it, _):
                    for t in range(K):
                        last = three(mm1[s][:, t * N:(t + 1) * N],
                                     lambda a, k: (wkh, wkl)[a][:, k, t * P:(t + 1) * P], h_all(s))
                    last.then_inc(qkv_up[s], 1)

                def v(s, it, _):
                    for t in range(T):
                        last = three(probb[s][:, t * D:(t + 1) * D], h_tile(s, t), lambda b, k: (wvh, wvl)[b][:, k, :])
                    last.then_inc(qkv_up[s], 1)

                def score(s, it, h):
                    if h < 2:
                        wait(pe, qs_up[s], it, 1, 1)
                        wait(pe, ks_up[s], it, 1, 1)
                    else:
                        wait(pe, smax_up[s], it, H3, h - 1)
                    o, r = (h * DH) // P, (h * DH) % P
                    for t in range(T):
                        last = pe.matmul(mmb[s][h % 2][:, t * N:(t + 1) * N], QT[s][r:r + DH, o, t * P:(t + 1) * P],
                                         KT[s][r:r + DH, o, :], start=True, stop=True)
                    last.then_inc(score_up[s], 1)

                def spturn(s, it, h):
                    if h == 0:
                        wait(pe, vs_up[s], it, 1, 1)
                    pturn(s, it, GATS + h)

                def smix(s, it, h):
                    wait(pe, pvals_up[s], it, ROUNDS, GATS + h + 1)
                    if h:
                        wait(pe, o_up[s], it, H3, h)
                    for t in range(T):
                        for j in range(T):
                            last = pe.matmul(turnb[s][:, t * DH:(t + 1) * DH], PT[s][:, j, t * P:(t + 1) * P],
                                             VV[s][:, j, h * DH:(h + 1) * DH], start=(j == 0), stop=(j == T - 1))
                    last.then_inc(mixed[s], 1)

                def oturn(s, it, _):
                    wait(pe, o_up[s], it, H3, H3)
                    for k in range(K):
                        for t in range(T):
                            last = pe.transpose(probb[s][:, k * N + t * P:k * N + (t + 1) * P],
                                                O3[s][:, t, k * P:(k + 1) * P], ident[:, :])
                    last.then_inc(oturned[s], 1)

                def wo(s, it, _):
                    wait(pe, oT_up[s], it, 1, 1)
                    for t in range(T):
                        for k in range(K):
                            last = pe.matmul(mm0[s][:, t * D:(t + 1) * D], OT[s][:, k, t * P:(t + 1) * P], woT[:, k, :],
                                             start=(k == 0), stop=(k == K - 1))
                    last.then_inc(wo_up[s], 1)

                walk(pe, {"turn": turn, "proj": proj, "sdp": sdp, "dst": dst, "pturn": pturn, "mix": mix,
                          "eturn": eturn, "up": up, "down": down, "msg": msg, "nbr": nbr, "q": q, "k": k_, "v": v,
                          "score": score, "spturn": spturn, "smix": smix, "oturn": oturn, "wo": wo})


_INS = ['x', 'adj', 'L0_gnn_W', 'L0_gnn_a_src', 'L0_gnn_a_dst', 'L1_gnn_W_heads', 'L1_gnn_a_heads', 'L1_gnn_W_out',
        'L1_gnn_a_out', 'L1_gnn_w1', 'L1_gnn_b1', 'L1_gnn_w2', 'L1_gnn_b2', 'L1_gnn_ln_gamma', 'L1_gnn_ln_beta',
        'L2_gnn_W', 'L2_gnn_b', 'L3_gnn_Wq', 'L3_gnn_bq', 'L3_gnn_Wk', 'L3_gnn_bk', 'L3_gnn_Wv', 'L3_gnn_bv',
        'L3_gnn_Wo', 'L3_gnn_bo']


def kernel(**inputs):
    import numpy as _np
    import concourse.bacc as _bacc
    from concourse import mybir as _mybir
    from concourse.bass_utils import run_bass_kernel_spmd as _run

    nc = _bacc.Bacc("TRN2", target_bir_lowering=False, num_devices=1)
    arrays, args = {}, []
    for name in _INS:
        a = _np.ascontiguousarray(inputs[name])
        arrays[f"in_{name}"] = a
        args.append(nc.dram_tensor(f"in_{name}", a.shape, _mybir.dt.from_np(a.dtype), kind="ExternalInput").ap())
    out = nc.dram_tensor("out_dram", (NB, N, D), _mybir.dt.float32, kind="ExternalOutput").ap()
    build(nc, *args, out)
    r = _run(nc, [arrays], core_ids=[0])
    return r.results[0]["out_dram"]
```

```python
from contextlib import ExitStack

import concourse.bass as bass
from concourse import mybir

f32 = mybir.dt.float32
f32r = mybir.dt.float32r
i32 = mybir.dt.int32
ALU = mybir.AluOpType
ACT = mybir.ActivationFunctionType
AX = mybir.AxisListType

P = 128
NB, N, D = 32, 256, 256
T = N // P
K = D // P
H1 = 4
H3 = 8
DH = D // H3
SLOTS = 4
ITERS = NB // SLOTS
EPS = 1e-5
MASKED = -1e30
SLOPE = [0.2] + [0.01] * (H1 + 1)
GATS = 2 + H1
ROUNDS = GATS + H3
SCALE = float(DH) ** -0.5
LN0, LN1, LNF, LN2, LN3 = range(5)
NLN = 5
TURN = {LN0: 0, LN1: 1, LN2: 2, LN3: 3}


def slot_steps():
    def norm(n):
        out = [("stats", n), ("coef", n), ("norm", n)]
        return out + ([("turn", n), ("hi", n), ("lo", n)] if n in TURN else [])

    def soften(g):
        return [("dst", g), ("dmax", g), ("leak", g), ("logit", g), ("prob", g)]

    def mix(g):
        return [("pturn", g), ("pvals", g), ("mix", g)]

    def elu(e):
        return [("expo", e), ("elu", e), ("eturn", e), ("eT", e)]

    first = norm(LN0) + [("proj", 0), ("vals", 0), ("sd", 0)] + soften(0) + mix(0) + [("x0", 0)]
    first += norm(LN1)
    for p in range(1, 5):
        first += [("proj", p), ("vals", p)]
    first += [("sdp", 0), ("sd", 1)]
    first += soften(1)
    for h in range(H1):
        if h + 1 < H1:
            a, b = soften(h + 2), mix(h + 1) + elu(h)
            first += [a[0], a[1], b[0], a[2], b[1], a[3], b[2], a[4], *b[3:]]
        else:
            first += mix(h + 1) + elu(h)
    second = [("proj", 5), ("vals", 5), ("sd", 2)] + soften(5) + mix(5) + elu(H1)
    second += [("up", 0), ("relu", 0), ("down", 0), ("ysum", 0)] + norm(LNF) + [("gain", 0), ("x1", 0)]
    second += norm(LN2) + [("msg", 0), ("mhi", 0), ("mlo", 0), ("self", 0), ("nbr", 0), ("x2", 0)]
    second += norm(LN3) + [("q", 0), ("k", 0), ("qs", 0), ("ks", 0), ("v", 0), ("vs", 0)]
    second += [("score", 0), ("smax", 0), ("sprob", 0)]
    for h in range(H3):
        a = [("score", h + 1), ("smax", h + 1), ("sprob", h + 1)] if h + 1 < H3 else []
        b = [("spturn", h), ("spvals", h), ("smix", h), ("onorm", h)]
        second += [x for pair in zip(a + [None], b) for x in pair if x] if a else b
    second += [("oturn", 0), ("oT", 0), ("wo", 0), ("done", 0)]
    return first, second


def merge(lists):
    at = [(( i + 0.5) / len(one), n, i) for n, one in enumerate(lists) for i in range(len(one))]
    return [lists[n][i] for _, n, i in sorted(at)]


def build(nc, x, adj, W0, a0s, a0d, W1, a1, WO1, aO1, w1, b1, w2, b2, gam, bet, W2, b2g,
          Wq, bq, Wk, bk, Wv, bv, Wo, bo, out):
    with ExitStack() as ctx:
        def sb(name, shape, dt=f32):
            return ctx.enter_context(nc.sbuf_tensor(name, [P, *shape], dt))

        def sem(name):
            return ctx.enter_context(nc.semaphore(name))

        def per_slot(name, shape, dt=f32):
            return [sb(f"{name}{s}", shape, dt) for s in range(SLOTS)]

        def sems(name):
            return [sem(f"{name}{s}") for s in range(SLOTS)]

        ident = sb("ident", [P])
        w0h, w0l = sb("w0h", [K, D + 2], f32r), sb("w0l", [K, D + 2], f32r)
        w1h, w1l = sb("w1h", [K, H1 * D], f32r), sb("w1l", [K, H1 * D], f32r)
        a1h, a1l = sb("a1h", [K, 2 * H1], f32r), sb("a1l", [K, 2 * H1], f32r)
        wout = sb("wout", [H1 * K, D + 2])
        wup, wdown = sb("wup", [K, D]), sb("wdown", [K, D])
        w2h, w2l = sb("w2h", [K, 2 * D], f32r), sb("w2l", [K, 2 * D], f32r)
        wqh, wql = sb("wqh", [K, D], f32r), sb("wql", [K, D], f32r)
        wkh, wkl = sb("wkh", [K, D], f32r), sb("wkl", [K, D], f32r)
        wvh, wvl = sb("wvh", [K, D], f32r), sb("wvl", [K, D], f32r)
        woT = sb("woT", [K, D])
        mask = sb("mask", [T, N])
        adjT = sb("adjT", [T, N], f32r)
        deg = sb("deg", [T])
        linked = sb("linked", [T])
        degb = sb("degb", [T, D])
        ffnb = sb("ffnb", [D])
        gamb, betb, bob = sb("gamb", [D]), sb("betb", [D]), sb("bob", [D])
        bcol = sb("bcol", [4 * K])
        b1c, bqc, bkc, bvc = (bcol[:, K * j:K * j + K] for j in range(4))
        minus_half, zero = sb("minus_half", [T]), sb("zero", [T])

        X = per_slot("X", [T, D])
        HN = per_slot("HN", [T, D])
        HH, HL = per_slot("HH", [K, N], f32r), per_slot("HL", [K, N], f32r)
        ST, MV = per_slot("ST", [T, 6]), per_slot("MV", [T, 2])
        VE, NM, RS, NMR = (per_slot(n, [T]) for n in ("VE", "NM", "RS", "NMR"))
        VAL = per_slot("VAL", [T, H1 * D])
        SD = per_slot("SD", [T, 2 * H1])
        NAS = per_slot("NAS", [T, H1])
        SMX = [per_slot(f"SMX{j}_", [T]) for j in range(2)]
        NDM, U, NMX = per_slot("NDM", [T]), per_slot("U", [T]), per_slot("NMX", [T])
        LG = per_slot("LG", [T, N])
        LK = per_slot("LK", [T, N])
        PR = per_slot("PR", [T, N])
        PT = per_slot("PT", [T, N])
        SUM = [per_slot(f"SUM{j}_", [T]) for j in range(2)]
        RI = [per_slot(f"RI{j}_", [T]) for j in range(2)]
        EL = per_slot("EL", [T, D])
        ET = per_slot("ET", [H1 * K, N])
        EX, F1, Y = HN, PT, LK
        MH, ML = HH, HL
        XB = EL
        OT = [v[:, 0:K, :] for v in ET]
        XO = [v[:, K:2 * K, :] for v in ET]
        SG = [LG, LK]
        QT = [v[:, :, 0:N] for v in VAL]
        KT = [v[:, :, N:2 * N] for v in VAL]
        VV = [v[:, :, 2 * N:3 * N] for v in VAL]
        O3 = [v[:, :, 3 * N:4 * N] for v in VAL]

        def banks(name):
            return [ctx.enter_context(nc.psum_tensor(f"{name}{s}", [P, 512], f32)) for s in range(SLOTS)]
        bankA, bankB = banks("bankA"), banks("bankB")
        AB = [[bankA[s], bankB[s]] for s in range(SLOTS)]

        def s_bank(s, h):
            return AB[s][1 - h % 2]

        def t_bank(s, h):
            return AB[s][1 - h % 2]

        HN_BANK = {LN0: 0, LN1: 1, LN2: 0, LN3: 1}

        def dst_bank(s, g):
            return AB[s][1 if g == 1 else 0]

        def m_bank(s, h):
            return AB[s][h % 2]

        def two(ap):
            return ap[:, :].rearrange("p (t n) -> p t n", t=2)

        w_in = [sem(f"w_in{j}") for j in range(4)]
        set_dve, set_pool, set_pe = sem("set_dve"), sem("set_pool"), sem("set_pe")
        reducing = sem("reducing")
        x_in, stored = sems("x_in"), sems("stored")
        stats, coef_up, normed = sems("stats"), sems("coef_up"), sems("normed")
        turned, hi_up, lo_up = sems("turned"), sems("hi_up"), sems("lo_up")
        dst_up, dmax_up, leak_up, logit_up = (sems(n) for n in ("dst_up", "dmax_up", "leak_up", "logit_up"))
        prob_up, pturned, pvals_up, mixed = sems("prob_up"), sems("pturned"), sems("pvals_up"), sems("mixed")
        rinv_up, score_up, smax_up, o_up = sems("rinv_up"), sems("score_up"), sems("smax_up"), sems("o_up")
        expo_up, elu_up, eturned, eT_up = sems("expo_up"), sems("elu_up"), sems("eturned"), sems("eT_up")
        xb_up, side_up, done = sems("xb_up"), sems("side_up"), sems("done")
        product = sems("product")
        moved = sems("moved")
        taken = sems("taken")

        PROJ0, PROJ1, PARTS, PROJ5, UP, DOWN, MSG, NBR, Q, KEY, V, WO = 1, 2, 6, 7, 8, 9, 10, 11, 12, 13, 14, 15
        PRODUCTS = 15
        M_VAL0, M_VAL1, M_VAL5, M_RELU, M_MSG, M_Q, M_V, M_O, MOVES = 1, 2, 6, 7, 8, 9, 10, 11, 11
        T_SD0, T_SD1, T_SD5, T_MSG, T_OWN, T_KEY, TAKES = 1, 2, 3, 4, 5, 6, 6

        first, second = slot_steps()
        GA, GB = list(range(SLOTS // 2)), list(range(SLOTS // 2, SLOTS))

        def tag(steps, group, late):
            return [[(name, s, late, arg) for name, arg in steps] for s in group]

        def walk(eng, handlers):
            def run(steps, it):
                for name, s, late, arg in steps:
                    if name in handlers:
                        handlers[name](s, it + late if late else it, arg)
            run(merge(tag(first, GA, 0)), 0)
            with eng.Fori(0, ITERS - 1) as it:
                run(merge(tag(second, GA, 0) + tag(first, GB, 0)), it)
                run(merge(tag(first, GA, 1) + tag(second, GB, 0)), it)
            run(merge(tag(second, GA, 0) + tag(first, GB, 0)), ITERS - 1)
            run(merge(tag(second, GB, 0)), ITERS - 1)

        def wait(eng, s_, it, per_pass, n):
            eng.wait_ge(s_, it * per_pass + n)

        raw = {n: ET[0][:, 2 * j:2 * j + 2, :] for j, n in enumerate(("Wq", "Wk", "Wv", "Wo"))}
        raw2 = VAL[0][:, 0:2, 0:2 * D]
        raw0 = VAL[0][:, :, 2 * D:3 * D]
        raw1 = VAL[1][:, :, :]
        adji = PR[0][:, :, :].bitcast(i32)
        adjf = PR[1]
        av = ET[1]
        junk = LK[0]
        brow = LK[1][:, 0, 0:P]
        a0b = EL[0]
        aOb = EL[1]

        WA, WA1 = sb("WA", [K, 2]), sb("WA1", [K, 2 * H1])
        whole = slice(0, D)
        TURNS = [(adjT, None, whole), (wqh, wql, whole), (wkh, wkl, whole), (wvh, wvl, whole),
                 (w2h, w2l, slice(0, D)), (w2h, w2l, slice(D, 2 * D)), (woT, None, whole)]
        TURN_SRC = [adjf[:, :, :], raw["Wq"], raw["Wk"], raw["Wv"], raw2[:, :, 0:D], raw2[:, :, D:2 * D], raw["Wo"]]
        TURN_MARKS = [17, 19, 21, 23, 25, 27, 28]
        SET_ALL = 29
        turn_marks = []
        w_counts = []

        with nc.Block() as block:
            @block.sync
            def _(sp):
                def bc(v):
                    return v.partition_broadcast(P)
                g0 = [(adji, adj.rearrange("(t p) n -> p t n", p=P)),
                      (wup[:, :, :], w1.rearrange("(t p) n -> p t n", p=P)),
                      (wdown[:, :, :], w2.rearrange("(t p) n -> p t n", p=P)),
                      (wout[:, :, 0:D], WO1.rearrange("(t p) n -> p t n", p=P))]
                g1 = [(raw0, W0.rearrange("(t p) n -> p t n", p=P)),
                      (a0b[:, 0, :], bc(a0s)), (a0b[:, 1, :], bc(a0d)),
                      (aOb[:, 0, :], bc(aO1[0:D])), (aOb[:, 1, :], bc(aO1[D:2 * D]))]
                g1 += [(raw1[:, :, h * D:(h + 1) * D], W1[h].rearrange("(t p) n -> p t n", p=P)) for h in range(H1)]
                g1 += [(av[:, 2 * h + j, :], bc(a1[h, j * D:(j + 1) * D])) for h in range(H1) for j in range(2)]
                g2 = [(raw[n], w.rearrange("(t p) n -> p t n", p=P))
                      for n, w in (("Wq", Wq), ("Wk", Wk), ("Wv", Wv), ("Wo", Wo))]
                g2 += [(raw2, W2.rearrange("(t p) n -> p t n", p=P))]
                g3 = [(degb[:, 0, :], bc(b2g)), (degb[:, 1, :], bc(b2g)), (ffnb[:, :], bc(b2)),
                      (gamb[:, :], bc(gam)), (betb[:, :], bc(bet)), (bob[:, :], bc(bo))]
                g3 += [(brow[2 * j:2 * j + 2, :], v.rearrange("(t p) -> t p", p=P)) for j, v in enumerate((b1, bq, bk, bv))]
                for j, g in enumerate((g0, g1, g2, g3)):
                    for dst, src in g:
                        sp.dma_start(dst, src).then_inc(w_in[j], 16)
                w_counts.extend(16 * len(g) for g in (g0, g1, g2, g3))

                def rows(dram, it, s):
                    return dram[bass.ds(it * SLOTS + s, 1), :, :].rearrange("a (t p) d -> p (a t) d", p=P)

                for s in range(SLOTS):
                    sp.dma_start(X[s][:, :, :], rows(x, 0, s)).then_inc(x_in[s], 16)
                with sp.Fori(0, ITERS - 1) as it:
                    for s in range(SLOTS):
                        wait(sp, xb_up[s], it, 3, 3)
                        wait(sp, normed[s], it, NLN, NLN)
                        sp.dma_start(X[s][:, :, :], rows(x, it + 1, s)).then_inc(x_in[s], 16)
                        wait(sp, done[s], it, 1, 1)
                        sp.dma_start(rows(out, it, s), XO[s]).then_inc(stored[s], 16)
                for s in range(SLOTS):
                    wait(sp, done[s], ITERS - 1, 1, 1)
                    sp.dma_start(rows(out, ITERS - 1, s), XO[s]).then_inc(stored[s], 16)
                for s in range(SLOTS):
                    sp.wait_ge(stored[s], 16 * ITERS + 1)

            @block.gpsimd
            def _(pool):
                pool.memset(ident[:, :], 0.0).then_inc(set_pool, 1)
                pool.memset(minus_half[:, :], -0.5).then_inc(set_pool, 1)
                pool.memset(zero[:, :], 0.0).then_inc(set_pool, 1)
                pool.wait_ge(set_pool, 3)
                pool.affine_select(out=ident[:, :], in_=ident[:, :], compare_op=ALU.not_equal, fill=1.0,
                                   base=0, pattern=[[-1, P]], channel_multiplier=1).then_inc(set_pool, 1)
                pool.wait_ge(set_dve, SET_ALL)

                def coef(s, it, n):
                    wait(pool, stats[s], it, NLN, n + 1)
                    pool.tensor_tensor(NM[s][:, :], zero[:, :], MV[s][:, :, 0], ALU.subtract)
                    pool.tensor_scalar(VE[s][:, :], MV[s][:, :, 1], EPS, 1.0, ALU.add, ALU.mult)
                    pool.drain()
                    pool.tensor_tensor(RS[s][:, :], VE[s][:, :], minus_half[:, :], ALU.pow)
                    pool.drain()
                    pool.tensor_tensor(NMR[s][:, :], NM[s][:, :], RS[s][:, :], ALU.mult).then_inc(coef_up[s], 1)
                    if n == LN2:
                        add_bias(s, it, 1)
                    if n == LN3:
                        add_bias(s, it, 2)

                def add_bias(s, it, j):
                    for t in range(T):
                        b = (betb[:, :], degb[:, t, :], bob[:, :])[j]
                        ins = pool.tensor_tensor(XB[s][:, t, :], X[s][:, t, :], b, ALU.add)
                    ins.then_inc(xb_up[s], 1)

                def gb(s, it, _):
                    wait(pool, eturned[s], it, H1 + 1, H1 + 1)
                    for t in range(T):
                        ins = pool.tensor_tensor(EL[s][:, t, :], EL[s][:, t, :], ffnb[:, :], ALU.add)
                    ins.then_inc(side_up[s], 1)

                def gain(s, it, _):
                    wait(pool, normed[s], it, NLN, LNF + 1)
                    for t in range(T):
                        ins = pool.tensor_tensor(Y[s][:, t, :], HN[s][:, t, :], gamb[:, :], ALU.mult)
                    ins.then_inc(side_up[s], 1)
                    add_bias(s, it, 0)

                walk(pool, {"coef": coef, "up": gb, "gain": gain})

            @block.scalar
            def _(act):
                act.wait_ge(set_dve, SET_ALL)

                def norm(s, it, n):
                    wait(act, coef_up[s], it, NLN, n + 1)
                    f = ACT.Identity if n == LNF else ACT.Relu
                    src = Y if n == LNF else X
                    for t in range(T):
                        ins = act.activation(HN[s][:, t, :], src[s][:, t, :], f, bias=NMR[s][:, t:t + 1],
                                             scale=RS[s][:, t:t + 1])
                    ins.then_inc(normed[s], 1)

                def hi(s, it, n):
                    wait(act, turned[s], it, 5, TURN[n] + 1)
                    act.activation(HH[s][:, :, :], two(AB[s][HN_BANK[n]]), ACT.Copy).then_inc(hi_up[s], 1)

                def vals(s, it, p):
                    wait(act, product[s], it, PRODUCTS, PROJ5 if p == 5 else PROJ0 + p)
                    if p in (0, 5):
                        for t in range(T):
                            ins = act.activation(VAL[s][:, t, 0:D], AB[s][t][:, 0:D], ACT.Copy)
                    else:
                        t, c = (p - 1) // 2, (p - 1) % 2
                        ins = act.activation(VAL[s][:, t, c * 512:(c + 1) * 512], AB[s][(p - 1) % 2][:, :], ACT.Copy)
                    ins.then_inc(moved[s], 1)

                def leak(s, it, g):
                    wait(act, dmax_up[s], it, GATS, g + 1)
                    h = g - 1 if 1 <= g <= H1 else 0
                    for t in range(T):
                        ins = act.activation(LK[s][:, t, :], LG[s][:, t, :], ACT.Identity,
                                             bias=NAS[s][:, t, h:h + 1], scale=SLOPE[g])
                    ins.then_inc(leak_up[s], 1)

                def prob(s, it, g):
                    wait(act, logit_up[s], it, GATS, g + 1)
                    for t in range(T):
                        ins = act.activation(PR[s][:, t, :], LG[s][:, t, :], ACT.Exp,
                                             bias=NMX[s][:, t:t + 1], scale=-1.0, accum_out=SUM[g % 2][s][:, t:t + 1])
                    ins.then_inc(prob_up[s], 1)

                def sprob(s, it, h):
                    wait(act, smax_up[s], it, H3, h + 1)
                    r = GATS + h
                    for t in range(T):
                        ins = act.activation(PR[s][:, t, :], SG[h % 2][s][:, t, :], ACT.Exp,
                                             bias=SMX[h % 2][s][:, t:t + 1], scale=-1.0,
                                             accum_out=SUM[r % 2][s][:, t:t + 1])
                    ins.then_inc(prob_up[s], 1)

                def pvals(s, it, r):
                    wait(act, pturned[s], it, ROUNDS, r + 1)
                    bank = bankB[s] if r < GATS else t_bank(s, r - GATS)
                    act.activation(PT[s][:, :, :], two(bank), ACT.Copy).then_inc(pvals_up[s], 1)

                def expo(s, it, e):
                    wait(act, rinv_up[s], it, ROUNDS, e + 2)
                    wait(act, mixed[s], it, ROUNDS, e + 2)
                    g = e + 1
                    for t in range(T):
                        ins = act.activation(EX[s][:, t, :], bankA[s][:, t * D:(t + 1) * D], ACT.Exp,
                                             scale=RI[g % 2][s][:, t:t + 1])
                    ins.then_inc(expo_up[s], 1)

                def relu(s, it, _):
                    wait(act, product[s], it, PRODUCTS, UP)
                    for t in range(K):
                        ins = act.activation(F1[s][:, t, :], bankA[s][:, t * N:(t + 1) * N], ACT.Relu, bias=b1c[:, t:t + 1])
                    ins.then_inc(moved[s], 1)

                def mhi(s, it, _):
                    wait(act, product[s], it, PRODUCTS, MSG)
                    for t in range(T):
                        ins = act.activation(MH[s][:, t, :], AB[s][t][:, D:2 * D], ACT.Copy)
                    ins.then_inc(moved[s], 1)

                def qs(s, it, _):
                    wait(act, product[s], it, PRODUCTS, Q)
                    for t in range(K):
                        ins = act.activation(QT[s][:, t, :], bankA[s][:, t * N:(t + 1) * N], ACT.Identity, bias=bqc[:, t:t + 1])
                    ins.then_inc(moved[s], 1)

                def vs(s, it, _):
                    wait(act, product[s], it, PRODUCTS, V)
                    act.activation(VV[s], two(bankA[s]), ACT.Copy).then_inc(moved[s], 1)

                def oT(s, it, _):
                    wait(act, turned[s], it, 5, 5)
                    act.activation(OT[s], two(bankA[s]), ACT.Copy).then_inc(moved[s], 1)

                walk(act, {"norm": norm, "hi": hi, "vals": vals, "leak": leak, "prob": prob, "sprob": sprob,
                           "pvals": pvals, "spvals": lambda s, it, h: pvals(s, it, GATS + h), "expo": expo,
                           "relu": relu, "mhi": mhi, "qs": qs, "vs": vs, "oT": oT})

            @block.vector
            def _(dve):
                count = [0]

                def mark(ins):
                    count[0] += 1
                    ins.then_inc(set_dve, 1)

                def split(hi, lo, src):
                    mark(dve.tensor_copy(hi, src))
                    dve.wait_ge(set_dve, count[0])
                    mark(dve.tensor_tensor(lo, src, hi.bitcast(f32), ALU.subtract))

                dve.wait_ge(w_in[0], w_counts[0])
                mark(dve.tensor_copy(adjf[:, :, :], adji))
                dve.wait_ge(set_dve, count[0])
                mark(dve.tensor_scalar(mask[:, :, :], adjf[:, :, :], 0.0, MASKED, ALU.is_equal, ALU.mult))
                mark(dve.tensor_reduce(deg[:, :], adjf[:, :, :], AX.X, ALU.add))
                dve.wait_ge(set_dve, count[0])
                mark(dve.tensor_reduce(linked[:, :], adjf[:, :, :], AX.X, ALU.max))
                dve.wait_ge(w_in[3], w_counts[3])
                for t in range(T):
                    mark(dve.tensor_scalar(degb[:, t, :], degb[:, t, :], deg[:, t:t + 1], None, ALU.mult))
                mark(dve.tensor_scalar(ffnb[:, :], ffnb[:, :], -1.0, None, ALU.add))

                def dot(dst, rows, vec):
                    dve.tensor_tensor_reduce(out=junk[:, 0, :], in0=rows, in1=vec, scale=1.0, scalar=0.0,
                                             op0=ALU.mult, op1=ALU.add, accum_out=dst)
                    dve.drain()

                dve.wait_ge(w_in[1], w_counts[1])
                for t in range(K):
                    for j in range(2):
                        dot(WA[:, t, j:j + 1], raw0[:, t, :], a0b[:, j, :])
                        for h in range(H1):
                            dot(WA1[:, t, j * H1 + h:j * H1 + h + 1], raw1[:, t, h * D:(h + 1) * D], av[:, 2 * h + j, :])
                for t in range(H1 * K):
                    for j in range(2):
                        dot(wout[:, t, D + j:D + j + 1], wout[:, t, 0:D], aOb[:, j, :])
                split(w0h[:, :, 0:D], w0l[:, :, 0:D], raw0)
                split(w0h[:, :, D:D + 2], w0l[:, :, D:D + 2], WA[:, :, :])
                split(w1h[:, :, :], w1l[:, :, :], raw1)
                split(a1h[:, :, :], a1l[:, :, :], WA1[:, :, :])

                dve.wait_ge(set_pe, 1)
                mark(dve.tensor_copy(bcol[:, :], bankB[0][:, 0:4 * K]))
                n = 0
                for hi, lo, cols in TURNS:
                    n += 1
                    src = two(bankA[n % 2])
                    dve.wait_ge(set_pe, n + 1)
                    if hi is woT:
                        mark(dve.tensor_copy(woT[:, :, :], src))
                    elif hi is adjT:
                        mark(dve.tensor_copy(adjT[:, :, :], src))
                    else:
                        split(hi[:, :, cols], lo[:, :, cols], src)
                    turn_marks.append(count[0])
                dve.wait_ge(set_pe, n + 2)
                mark(dve.tensor_tensor(bob[:, :], bankB[1][:, 0:D], bob[:, :], ALU.add))
                assert count[0] == SET_ALL, count
                assert turn_marks == TURN_MARKS, turn_marks

                def stats_(s, it, n):
                    if n == LN0:
                        wait(dve, x_in[s], it, 16, 16)
                    src = Y if n == LNF else X
                    for t in range(T):
                        dve.bn_stats(ST[s][:, t, :], src[s][:, t, :])
                    dve.drain()
                    for t in range(T):
                        ins = dve.bn_aggr(MV[s][:, t, :], ST[s][:, t, :])
                    ins.then_inc(stats[s], 1)

                def lo(s, it, n):
                    wait(dve, hi_up[s], it, 4, TURN[n] + 1)
                    dve.tensor_tensor(HL[s][:, :, :], two(AB[s][HN_BANK[n]]), HH[s][:, :, :].bitcast(f32),
                                      ALU.subtract).then_inc(lo_up[s], 1)

                def sd(s, it, l):
                    heads = H1 if l == 1 else 1
                    if l == 1:
                        wait(dve, product[s], it, PRODUCTS, PARTS)
                        dve.tensor_copy(SD[s][:, :, :], bankA[s][:, 0:4 * H1].rearrange("p (t n) -> p t n", t=T))
                    else:
                        wait(dve, moved[s], it, MOVES, M_VAL5 if l else M_VAL0)
                        for t in range(T):
                            dve.tensor_copy(SD[s][:, t, 0:2], AB[s][t][:, D:D + 2])
                    dve.drain()
                    dve.tensor_scalar(NAS[s][:, :, 0:heads], SD[s][:, :, 0:heads], -SLOPE[l], None,
                                      ALU.mult).then_inc(taken[s], 1)

                def dmax(s, it, g):
                    wait(dve, dst_up[s], it, GATS, g + 1)
                    if g:
                        wait(dve, prob_up[s], it, ROUNDS, g)
                    h = g - 1 if 1 <= g <= H1 else 0
                    dve.sem_inc(reducing, 1)
                    for t in range(T):
                        ins = dve.tensor_tensor_reduce(out=LG[s][:, t, :], in0=dst_bank(s, g)[:, 0:N], in1=mask[:, t, :],
                                                       scale=-1.0, scalar=3.0e38, op0=ALU.add, op1=ALU.min,
                                                       accum_out=NDM[s][:, t:t + 1])
                    ins.then_inc(dmax_up[s], 1)
                    dve.drain()
                    dve.tensor_tensor(U[s][:, :], NDM[s][:, :], SD[s][:, :, h], ALU.subtract)
                    dve.drain()
                    dve.scalar_tensor_tensor(NMX[s][:, :], U[s][:, :], SLOPE[g], U[s][:, :], ALU.mult, ALU.min)

                def logit(s, it, g):
                    wait(dve, leak_up[s], it, GATS, g + 1)
                    h = g - 1 if 1 <= g <= H1 else 0
                    for t in range(T):
                        ins = dve.scalar_tensor_tensor(LG[s][:, t, :], LG[s][:, t, :], SD[s][:, t, h:h + 1],
                                                       LK[s][:, t, :], ALU.subtract, ALU.min)
                    ins.then_inc(logit_up[s], 1)

                def rinv(s, it, r):
                    wait(dve, prob_up[s], it, ROUNDS, r + 1)
                    ins = dve.reciprocal(RI[r % 2][s][:, :], SUM[r % 2][s][:, :])
                    if r == 0:
                        dve.drain()
                        ins = dve.tensor_tensor(RI[0][s][:, :], RI[0][s][:, :], linked[:, :], ALU.mult)
                    ins.then_inc(rinv_up[s], 1)

                def x0(s, it, _):
                    dve.drain()
                    wait(dve, mixed[s], it, ROUNDS, 1)
                    for t in range(T):
                        ins = dve.scalar_tensor_tensor(X[s][:, t, :], bankA[s][:, t * D:(t + 1) * D], RI[0][s][:, t:t + 1],
                                                       X[s][:, t, :], ALU.mult, ALU.add)
                    dve.drain()

                def elu(s, it, e):
                    g = e + 1
                    if e:
                        wait(dve, eturned[s], it, H1 + 1, e)
                    wait(dve, expo_up[s], it, H1 + 1, e + 1)
                    for t in range(T):
                        dve.tensor_scalar(EL[s][:, t, :], bankA[s][:, t * D:(t + 1) * D], RI[g % 2][s][:, t:t + 1],
                                          0.0, ALU.mult, ALU.max)
                    dve.drain()
                    dve.scalar_tensor_tensor(EL[s][:, :, :], EX[s][:, :, :], 1.0, EL[s][:, :, :], ALU.min,
                                             ALU.add).then_inc(elu_up[s], 1)

                def eT(s, it, e):
                    if e == 1:
                        dve.wait_ge(stored[s], it * 16 + 1)
                    wait(dve, eturned[s], it, H1 + 1, e + 1)
                    dst = OT[s] if e == H1 else ET[s][:, 2 * e:2 * e + 2, :]
                    dve.tensor_scalar(dst, two(bankB[s]), -1.0, None, ALU.add).then_inc(eT_up[s], 1)

                def ysum(s, it, _):
                    wait(dve, side_up[s], it, 2, 1)
                    wait(dve, product[s], it, PRODUCTS, DOWN)
                    dve.tensor_tensor(Y[s][:, :, :], two(bankB[s]), EL[s][:, :, :], ALU.add)
                    dve.drain()

                def x1(s, it, _):
                    wait(dve, xb_up[s], it, 3, 1)
                    wait(dve, side_up[s], it, 2, 2)
                    dve.tensor_tensor(X[s][:, :, :], Y[s][:, :, :], XB[s][:, :, :], ALU.add)
                    dve.drain()

                def mlo(s, it, _):
                    wait(dve, moved[s], it, MOVES, M_MSG)
                    for t in range(T):
                        ins = dve.tensor_tensor(ML[s][:, t, :], AB[s][t][:, D:2 * D], MH[s][:, t, :].bitcast(f32),
                                                ALU.subtract)
                    ins.then_inc(taken[s], 1)

                def own(s, it, _):
                    wait(dve, xb_up[s], it, 3, 2)
                    for t in range(T):
                        ins = dve.scalar_tensor_tensor(X[s][:, t, :], AB[s][t][:, 0:D], deg[:, t:t + 1],
                                                       XB[s][:, t, :], ALU.mult, ALU.add)
                    ins.then_inc(taken[s], 1)
                    dve.drain()

                def x2(s, it, _):
                    wait(dve, product[s], it, PRODUCTS, NBR)
                    dve.tensor_tensor(X[s][:, :, :], two(bankA[s]), X[s][:, :, :], ALU.add)
                    dve.drain()

                def ks(s, it, _):
                    wait(dve, product[s], it, PRODUCTS, KEY)
                    for t in range(K):
                        ins = dve.tensor_scalar(KT[s][:, t, :], bankB[s][:, t * N:(t + 1) * N], bkc[:, t:t + 1], None, ALU.add)
                    ins.then_inc(taken[s], 1)

                def smax(s, it, h):
                    wait(dve, score_up[s], it, H3, h + 1)
                    if h >= 2:
                        wait(dve, prob_up[s], it, ROUNDS, GATS + h - 1)
                    dve.sem_inc(reducing, 1)
                    for t in range(T):
                        ins = dve.tensor_tensor_reduce(out=SG[h % 2][s][:, t, :], in0=s_bank(s, h)[:, t * N:(t + 1) * N],
                                                       in1=mask[:, t, :], scale=-SCALE, scalar=3.0e38, op0=ALU.add,
                                                       op1=ALU.min, accum_out=SMX[h % 2][s][:, t:t + 1])
                    ins.then_inc(smax_up[s], 1)

                def onorm(s, it, h):
                    r = GATS + h
                    rinv(s, it, r)
                    dve.drain()
                    wait(dve, mixed[s], it, ROUNDS, r + 1)
                    for t in range(T):
                        ins = dve.tensor_scalar(O3[s][:, t, h * DH:(h + 1) * DH], m_bank(s, h)[:, t * DH:(t + 1) * DH],
                                                RI[r % 2][s][:, t:t + 1], None, ALU.mult)
                    ins.then_inc(o_up[s], 1)

                def finish(s, it, _):
                    wait(dve, xb_up[s], it, 3, 3)
                    wait(dve, product[s], it, PRODUCTS, WO)
                    dve.tensor_tensor(XO[s], two(bankB[s]), XB[s][:, :, :], ALU.add).then_inc(done[s], 1)

                for s in range(SLOTS):
                    dve.sem_inc(stored[s], 1)
                walk(dve, {"stats": stats_, "lo": lo, "sd": sd, "dmax": dmax, "logit": logit, "pvals": rinv, "x0": x0,
                           "elu": elu, "eT": eT, "ysum": ysum, "x1": x1, "mlo": mlo, "self": own, "x2": x2,
                           "ks": ks, "smax": smax, "onorm": onorm, "done": finish})

            @block.tensor
            def _(pe):
                pe.wait_ge(set_pool, 4)
                pe.wait_ge(w_in[2], w_counts[2])
                pe.wait_ge(set_dve, 1)
                pe.wait_ge(w_in[3], w_counts[3])
                pe.transpose(bankB[0][:, 0:4 * K], brow[0:4 * K, :], ident[0:4 * K, 0:4 * K]).then_inc(set_pe, 1)
                n = 0
                for hi, lo, cols in TURNS:
                    n += 1
                    if n > 2:
                        pe.wait_ge(set_dve, TURN_MARKS[n - 3])
                    for k in range(K):
                        for t in range(2):
                            src = TURN_SRC[n - 1][:, t, k * P:(k + 1) * P]
                            last = pe.transpose(bankA[n % 2][:, k * 256 + t * P:k * 256 + (t + 1) * P], src, ident[:, :])
                    last.then_inc(set_pe, 1)
                pe.wait_ge(set_dve, SET_ALL - 1)
                pe.wait_ge(w_in[3], w_counts[3])
                for k in range(K):
                    last = pe.matmul(bankB[1][:, 0:D], bvc[:, k:k + 1].to_broadcast([P, P]), woT[:, k, :],
                                     start=(k == 0), stop=(k == K - 1))
                last.then_inc(set_pe, 1)
                pe.wait_ge(set_dve, SET_ALL)

                def three(bank, stat, mov):
                    ops = [(k, a, b) for k in range(K) for a, b in ((0, 0), (0, 1), (1, 0))]
                    for n, (k, a, b) in enumerate(ops):
                        last = pe.matmul(bank, stat(a, k), mov(b, k), start=(n == 0), stop=(n == len(ops) - 1))
                    return last

                def turn(s, it, n):
                    wait(pe, normed[s], it, NLN, n + 1)
                    for k in range(K):
                        for t in range(T):
                            last = pe.transpose(AB[s][HN_BANK[n]][:, k * N + t * P:k * N + (t + 1) * P],
                                                HN[s][:, t, k * P:(k + 1) * P], ident[:, :])
                    last.then_inc(turned[s], 1)

                def h_tile(s, t):
                    return lambda a, k: (HH, HL)[a][s][:, k, t * P:(t + 1) * P]

                def h_all(s):
                    return lambda a, k: (HH, HL)[a][s][:, k, :]

                def proj(s, it, p):
                    if p == 0:
                        wait(pe, lo_up[s], it, 4, 1)
                        for t in range(T):
                            last = three(AB[s][t][:, 0:D + 2], h_tile(s, t), lambda b, k: (w0h, w0l)[b][:, k, :])
                    elif p == 5:
                        wait(pe, eT_up[s], it, H1 + 1, H1)
                        for t in range(T):
                            for k in range(H1 * K):
                                last = pe.matmul(AB[s][t][:, 0:D + 2], ET[s][:, k, t * P:(t + 1) * P], wout[:, k, :],
                                                 start=(k == 0), stop=(k == H1 * K - 1))
                    else:
                        if p == 1:
                            wait(pe, lo_up[s], it, 4, 2)
                        if p > 2:
                            wait(pe, moved[s], it, MOVES, M_VAL1 + p - 3)
                        t, c = (p - 1) // 2, (p - 1) % 2
                        last = three(AB[s][(p - 1) % 2][:, :], h_tile(s, t),
                                     lambda b, k: (w1h, w1l)[b][:, k, c * 512:(c + 1) * 512])
                    last.then_inc(product[s], 1)

                def sdp(s, it, _):
                    wait(pe, moved[s], it, MOVES, M_VAL1 + 2)
                    for t in range(T):
                        last = three(bankA[s][:, t * 2 * H1:(t + 1) * 2 * H1], h_tile(s, t),
                                     lambda b, k: (a1h, a1l)[b][:, k, :])
                    last.then_inc(product[s], 1)

                def dst(s, it, g):
                    wait(pe, taken[s], it, TAKES, T_SD0 if g == 0 else T_SD5 if g == 5 else T_SD1)
                    if g == 1:
                        wait(pe, moved[s], it, MOVES, M_VAL1 + 3)
                    if 3 <= g <= H1:
                        wait(pe, elu_up[s], it, H1 + 1, g - 2)
                    c = H1 + g - 1 if 1 <= g <= H1 else 1
                    for t in range(T):
                        last = pe.transpose(dst_bank(s, g)[:, t * P:(t + 1) * P], SD[s][:, t, c:c + 1].to_broadcast([P, P]),
                                            ident[:, :])
                    last.then_inc(dst_up[s], 1)

                def pturn(s, it, r):
                    wait(pe, prob_up[s], it, ROUNDS, r + 1)
                    bank = bankB[s] if r < GATS else t_bank(s, r - GATS)
                    if 2 <= r <= H1:
                        wait(pe, eT_up[s], it, H1 + 1, r - 1)
                    if r > GATS:
                        wait(pe, o_up[s], it, H3, r - GATS)
                    for j in range(T):
                        for t in range(T):
                            last = pe.transpose(bank[:, j * N + t * P:j * N + (t + 1) * P],
                                                PR[s][:, t, j * P:(j + 1) * P], ident[:, :])
                    last.then_inc(pturned[s], 1)

                def mix(s, it, g):
                    wait(pe, pvals_up[s], it, ROUNDS, g + 1)
                    if 1 <= g < H1:
                        wait(pe, dmax_up[s], it, GATS, g + 2)
                    if g == H1:
                        wait(pe, elu_up[s], it, H1 + 1, g - 1)
                    h = g - 1 if 1 <= g <= H1 else 0
                    for t in range(T):
                        for j in range(T):
                            last = pe.matmul(bankA[s][:, t * D:(t + 1) * D], PT[s][:, j, t * P:(t + 1) * P],
                                             VAL[s][:, j, h * D:(h + 1) * D], start=(j == 0), stop=(j == T - 1))
                    last.then_inc(mixed[s], 1)

                def eturn(s, it, e):
                    wait(pe, elu_up[s], it, H1 + 1, e + 1)
                    for k in range(K):
                        for t in range(T):
                            last = pe.transpose(bankB[s][:, k * N + t * P:k * N + (t + 1) * P],
                                                EL[s][:, t, k * P:(k + 1) * P], ident[:, :])
                    last.then_inc(eturned[s], 1)

                def up(s, it, _):
                    wait(pe, eT_up[s], it, H1 + 1, H1 + 1)
                    for t in range(K):
                        for k in range(K):
                            last = pe.matmul(bankA[s][:, t * N:(t + 1) * N], wup[:, k, t * P:(t + 1) * P], OT[s][:, k, :],
                                             start=(k == 0), stop=(k == K - 1))
                    last.then_inc(product[s], 1)

                def down(s, it, _):
                    wait(pe, moved[s], it, MOVES, M_RELU)
                    for t in range(T):
                        for k in range(K):
                            last = pe.matmul(bankB[s][:, t * D:(t + 1) * D], F1[s][:, k, t * P:(t + 1) * P], wdown[:, k, :],
                                             start=(k == 0), stop=(k == K - 1))
                    last.then_inc(product[s], 1)

                def msg(s, it, _):
                    wait(pe, lo_up[s], it, 4, 3)
                    for t in range(T):
                        last = three(AB[s][t][:, :], h_tile(s, t), lambda b, k: (w2h, w2l)[b][:, k, :])
                    last.then_inc(product[s], 1)

                def nbr(s, it, _):
                    wait(pe, taken[s], it, TAKES, T_OWN)
                    for t in range(T):
                        ops = [(j, m) for j in range(T) for m in (MH, ML)]
                        for n, (j, m) in enumerate(ops):
                            last = pe.matmul(bankA[s][:, t * D:(t + 1) * D], adjT[:, j, t * P:(t + 1) * P], m[s][:, j, :],
                                             start=(n == 0), stop=(n == len(ops) - 1))
                    last.then_inc(product[s], 1)

                def q(s, it, _):
                    wait(pe, lo_up[s], it, 4, 4)
                    for t in range(K):
                        last = three(bankA[s][:, t * N:(t + 1) * N],
                                     lambda a, k: (wqh, wql)[a][:, k, t * P:(t + 1) * P], h_all(s))
                    last.then_inc(product[s], 1)

                def k_(s, it, _):
                    for t in range(K):
                        last = three(bankB[s][:, t * N:(t + 1) * N],
                                     lambda a, k: (wkh, wkl)[a][:, k, t * P:(t + 1) * P], h_all(s))
                    last.then_inc(product[s], 1)

                def v(s, it, _):
                    wait(pe, moved[s], it, MOVES, M_Q)
                    for t in range(T):
                        last = three(bankA[s][:, t * D:(t + 1) * D], h_tile(s, t), lambda b, k: (wvh, wvl)[b][:, k, :])
                    last.then_inc(product[s], 1)

                def score(s, it, h):
                    if h == 0:
                        wait(pe, taken[s], it, TAKES, T_KEY)
                    elif h == 1:
                        wait(pe, moved[s], it, MOVES, M_V)
                    else:
                        wait(pe, pvals_up[s], it, ROUNDS, GATS + h - 1)
                    o, r = (h * DH) // P, (h * DH) % P
                    for t in range(T):
                        last = pe.matmul(s_bank(s, h)[:, t * N:(t + 1) * N], QT[s][r:r + DH, o, t * P:(t + 1) * P],
                                         KT[s][r:r + DH, o, :], start=True, stop=True)
                    last.then_inc(score_up[s], 1)

                def spturn(s, it, h):
                    pturn(s, it, GATS + h)

                def smix(s, it, h):
                    wait(pe, pvals_up[s], it, ROUNDS, GATS + h + 1)
                    if h + 1 < H3:
                        wait(pe, smax_up[s], it, H3, h + 2)
                    for t in range(T):
                        for j in range(T):
                            last = pe.matmul(m_bank(s, h)[:, t * DH:(t + 1) * DH], PT[s][:, j, t * P:(t + 1) * P],
                                             VV[s][:, j, h * DH:(h + 1) * DH], start=(j == 0), stop=(j == T - 1))
                    last.then_inc(mixed[s], 1)

                def oturn(s, it, _):
                    wait(pe, o_up[s], it, H3, H3)
                    for k in range(K):
                        for t in range(T):
                            last = pe.transpose(bankA[s][:, k * N + t * P:k * N + (t + 1) * P],
                                                O3[s][:, t, k * P:(k + 1) * P], ident[:, :])
                    last.then_inc(turned[s], 1)

                def wo(s, it, _):
                    wait(pe, moved[s], it, MOVES, M_O)
                    for t in range(T):
                        for k in range(K):
                            last = pe.matmul(bankB[s][:, t * D:(t + 1) * D], OT[s][:, k, t * P:(t + 1) * P], woT[:, k, :],
                                             start=(k == 0), stop=(k == K - 1))
                    last.then_inc(product[s], 1)

                walk(pe, {"turn": turn, "proj": proj, "sdp": sdp, "dst": dst, "pturn": pturn, "mix": mix,
                          "eturn": eturn, "up": up, "down": down, "msg": msg, "nbr": nbr, "q": q, "k": k_, "v": v,
                          "score": score, "spturn": spturn, "smix": smix, "oturn": oturn, "wo": wo})


_INS = ['x', 'adj', 'L0_gnn_W', 'L0_gnn_a_src', 'L0_gnn_a_dst', 'L1_gnn_W_heads', 'L1_gnn_a_heads', 'L1_gnn_W_out',
        'L1_gnn_a_out', 'L1_gnn_w1', 'L1_gnn_b1', 'L1_gnn_w2', 'L1_gnn_b2', 'L1_gnn_ln_gamma', 'L1_gnn_ln_beta',
        'L2_gnn_W', 'L2_gnn_b', 'L3_gnn_Wq', 'L3_gnn_bq', 'L3_gnn_Wk', 'L3_gnn_bk', 'L3_gnn_Wv', 'L3_gnn_bv',
        'L3_gnn_Wo', 'L3_gnn_bo']


def kernel(**inputs):
    import numpy as _np
    import concourse.bacc as _bacc
    from concourse import mybir as _mybir
    from concourse.bass_utils import run_bass_kernel_spmd as _run

    nc = _bacc.Bacc("TRN2", target_bir_lowering=False, num_devices=1)
    arrays, args = {}, []
    for name in _INS:
        a = _np.ascontiguousarray(inputs[name])
        arrays[f"in_{name}"] = a
        args.append(nc.dram_tensor(f"in_{name}", a.shape, _mybir.dt.from_np(a.dtype), kind="ExternalInput").ap())
    out = nc.dram_tensor("out_dram", (NB, N, D), _mybir.dt.float32, kind="ExternalOutput").ap()
    build(nc, *args, out)
    r = _run(nc, [arrays], core_ids=[0])
    return r.results[0]["out_dram"]
```

```python
from contextlib import ExitStack

import concourse.bass as bass
from concourse import mybir

f32 = mybir.dt.float32
f32r = mybir.dt.float32r
i32 = mybir.dt.int32
ALU = mybir.AluOpType
ACT = mybir.ActivationFunctionType
AX = mybir.AxisListType

P = 128
NB, N, D = 32, 256, 256
T = N // P
K = D // P
H1 = 4
H3 = 8
DH = D // H3
SLOTS = 4
ITERS = NB // SLOTS
EPS = 1e-5
MASKED = -1e30
SLOPE = [0.2] + [0.01] * (H1 + 1)
GATS = 2 + H1
ROUNDS = GATS + H3
SCALE = float(DH) ** -0.5
LN0, LN1, LNF, LN2, LN3 = range(5)
NLN = 5
TURN = {LN0: 0, LN1: 1, LN2: 2, LN3: 3}


STEPS = {"stats": ("D", 982), "coef": ("G", 1277), "norm": ("A", 986), "turn": ("P", 434), "hi": ("A", 478),
         "lo": ("D", 602), "proj": ("P", 1300), "vals": ("A", 478), "sdp": ("P", 786), "sd": ("D", 366),
         "dst": ("P", 216), "dmax": ("D", 1144, 770), "leak": ("A", 800), "logit": ("D", 792), "prob": ("A", 986),
         "pturn": ("P", 434), "pvals": ("A", 478), "rinv": ("D", 90), "mix": ("P", 1725), "x0": ("D", 930),
         "pnorm": ("D", 769), "expo": ("A", 478), "elu": ("D", 1099), "eturn": ("P", 434), "eT": ("D", 602),
         "up": ("P", 1725), "relu": ("A", 716), "gb": ("G", 2748, 1374), "down": ("P", 1725), "ysum": ("D", 694),
         "gain": ("G", 1374), "x1": ("D", 694), "msg": ("P", 2589), "mhi": ("A", 528), "mlo": ("D", 670),
         "self": ("D", 884), "nbr": ("P", 870), "x2": ("D", 694), "q": ("P", 1306), "k": ("P", 1306),
         "v": ("P", 1306), "qs": ("A", 716), "qlo": ("D", 784), "ks": ("D", 784), "klo": ("D", 854),
         "vs": ("A", 478), "score": ("P", 646), "smax": ("D", 686), "sprob": ("A", 986), "spturn": ("P", 434),
         "spvals": ("A", 478), "smix": ("P", 776), "onorm": ("D", 390), "oturn": ("P", 434), "oT": ("A", 478),
         "wo": ("P", 1725), "done": ("D", 602)}
LONG_STEPS = {("proj", 5): (6970,), ("vals", 0): (742,), ("vals", 5): (742,), ("expo", H1): (716,),
              ("elu", H1): (1548,), ("coef", LN2): (2651, 1277), ("coef", LN3): (2651, 1277)}
HOP = {"PA": 197, "PD": 250, "PG": 224, "AD": 120, "AP": 270, "AG": 170, "DP": 250, "DA": 110, "DG": 155,
       "GA": 75, "GD": 74}
ISSUE = {"P": 20, "A": 30, "D": 50, "G": 60}
AHEAD = (0, 0.171, 0.351, 0.473)
FAVOUR = (0, -4155, -4474, -5360)


def times(step):
    t = LONG_STEPS.get(step, STEPS[step[0]][1:])
    return t[0], t[-1]


def delay(step, then):
    return times(step)[1] + HOP.get(STEPS[step[0]][0] + STEPS[then[0]][0], 0)


def pass_steps():
    after = {}

    def add(step, *before):
        after[step] = [b for b in before if b]

    def norm(n, x):
        add(("stats", n), x)
        add(("coef", n), ("stats", n))
        add(("norm", n), ("coef", n))
        if n in TURN:
            add(("turn", n), ("norm", n))
            add(("hi", n), ("turn", n))
            add(("lo", n), ("hi", n))

    def soften(g, *before):
        inner = 1 < g <= H1
        add(("dst", g), ("dst", g - 1) if inner else None, ("pvals", g - 2) if inner and g > 2 else None, *before)
        add(("dmax", g), ("dst", g), ("prob", g - 1) if inner else None)
        add(("leak", g), ("dmax", g))
        add(("logit", g), ("leak", g))
        add(("prob", g), ("logit", g), ("pturn", g - 1) if inner else None)

    def mix(g, *before):
        r = ("pnorm" if 1 <= g <= H1 else "rinv", g)
        add(r, ("prob", g))
        add(("pturn", g), r if 1 <= g <= H1 else ("prob", g), *before)
        add(("pvals", g), ("pturn", g))
        add(("mix", g), ("pvals", g), ("dmax", g + 1) if 1 <= g < H1 else None)

    def elu(e):
        add(("expo", e), ("mix", e + 1), ("rinv", e + 1) if e == H1 else None)
        add(("elu", e), ("expo", e))
        if e == H1:
            add(("eturn", e), ("elu", e))
            add(("eT", e), ("eturn", e))

    norm(LN0, None)
    add(("proj", 0), ("lo", LN0))
    add(("vals", 0), ("proj", 0))
    add(("sd", 0), ("vals", 0))
    soften(0, ("sd", 0))
    mix(0)
    add(("x0", 0), ("mix", 0), ("rinv", 0))
    norm(LN1, ("x0", 0))
    for p in range(1, 5):
        add(("proj", p), ("lo", LN1), ("proj", p - 1), ("vals", p - 2) if p > 2 else None)
        add(("vals", p), ("proj", p))
    add(("sdp", 0), ("vals", 3), ("proj", 4))
    add(("sd", 1), ("sdp", 0))
    soften(1, ("sd", 1), ("vals", 4))
    for h in range(H1):
        if h + 1 < H1:
            soften(h + 2, ("sd", 1))
        mix(h + 1, ("elu", h - 1) if h else None)
        elu(h)
    add(("proj", 5), ("elu", H1 - 1))
    add(("vals", 5), ("proj", 5))
    add(("sd", 2), ("vals", 5))
    soften(5, ("sd", 2))
    mix(5)
    elu(H1)
    add(("up", 0), ("eT", H1))
    add(("relu", 0), ("up", 0))
    add(("gb", 0), ("eturn", H1))
    add(("down", 0), ("relu", 0))
    add(("ysum", 0), ("down", 0), ("gb", 0))
    norm(LNF, ("ysum", 0))
    add(("gain", 0), ("norm", LNF))
    add(("x1", 0), ("gain", 0))
    norm(LN2, ("x1", 0))
    add(("msg", 0), ("lo", LN2))
    add(("mhi", 0), ("msg", 0))
    add(("mlo", 0), ("mhi", 0))
    add(("self", 0), ("mlo", 0))
    add(("nbr", 0), ("self", 0))
    add(("x2", 0), ("nbr", 0))
    norm(LN3, ("x2", 0))
    add(("q", 0), ("lo", LN3))
    add(("k", 0), ("q", 0))
    add(("qs", 0), ("q", 0))
    add(("qlo", 0), ("qs", 0))
    add(("ks", 0), ("k", 0), ("qlo", 0))
    add(("klo", 0), ("ks", 0))
    add(("v", 0), ("k", 0), ("qlo", 0))
    add(("vs", 0), ("v", 0))
    for h in range(-1, H3):
        j = h + 1
        if j < H3:
            add(("score", j), ("klo", 0), ("score", j - 1) if j else ("v", 0), ("vs", 0) if j == 1 else None,
                ("spvals", j - 2) if j > 1 else None)
            add(("smax", j), ("score", j), ("smax", j - 1) if j else None, ("sprob", j - 2) if j > 1 else None)
            add(("sprob", j), ("smax", j), ("spturn", j - 1) if j else None)
        if h >= 0:
            add(("spturn", h), ("sprob", h), ("onorm", h - 1) if h else None)
            add(("spvals", h), ("spturn", h))
            add(("rinv", GATS + h), ("sprob", h))
            add(("smix", h), ("spvals", h), ("smax", h + 1) if j < H3 else None)
            add(("onorm", h), ("smix", h), ("rinv", GATS + h))
    add(("oturn", 0), ("onorm", H3 - 1))
    add(("oT", 0), ("oturn", 0))
    add(("wo", 0), ("oT", 0))
    add(("done", 0), ("wo", 0))

    placed = {}

    def place(step):
        if step not in placed:
            for b in after[step]:
                place(b)
            placed[step] = after[step]

    for step in after:
        place(step)
    return placed


def interleave(after, items):
    here = set(items)
    before = {x: [(x[0], x[1], b) for b in after[x[2]]] +
                 ([(x[0], x[1] - 1, ("done", 0))] if x[2] == ("stats", 0) else []) for x in items}
    follow = {x: [] for x in items}
    for x in items:
        for b in before[x]:
            if b in here:
                follow[b].append(x)
    chain = {}
    for x in reversed(items):
        chain[x] = max([delay(x[2], y[2]) + chain[y] for y in follow[x]], default=times(x[2])[0])
    order = []
    free, began = dict.fromkeys("PDAG", 0), {}
    for rounds in range(3):
        missing = {x: sum(b in here for b in before[x]) for x in items}
        able = {e: {} for e in "PDAG"}

        def enable(x):
            able[STEPS[x[2][0]][0]][x] = max(
                [began[b[0], rounds + b[1], b[2]] + delay(b[2], x[2]) for b in before[x]
                 if (b[0], rounds + b[1], b[2]) in began], default=0)

        for x in items:
            if not missing[x]:
                enable(x)
        order = []
        for _ in items:
            start, e = min((max(free[e], min(able[e].values())), e) for e in "PDAG" if able[e])
            x = max((x for x in able[e] if able[e][x] <= start), key=lambda x: (chain[x] + FAVOUR[x[0]], -x[0]))
            del able[e][x]
            free[e] = start + times(x[2])[0] + ISSUE[e]
            began[x[0], rounds + x[1], x[2]] = start
            order.append((start, len(order), x))
            for y in follow[x]:
                missing[y] -= 1
                if not missing[y]:
                    enable(y)
    return [x for _, _, x in sorted(order)]


def build(nc, x, adj, W0, a0s, a0d, W1, a1, WO1, aO1, w1, b1, w2, b2, gam, bet, W2, b2g,
          Wq, bq, Wk, bk, Wv, bv, Wo, bo, out):
    with ExitStack() as ctx:
        def sb(name, shape, dt=f32):
            return ctx.enter_context(nc.sbuf_tensor(name, [P, *shape], dt))

        def sem(name):
            return ctx.enter_context(nc.semaphore(name))

        def per_slot(name, shape, dt=f32):
            return [sb(f"{name}{s}", shape, dt) for s in range(SLOTS)]

        def sems(name):
            return [sem(f"{name}{s}") for s in range(SLOTS)]

        ident = sb("ident", [P])
        w0h, w0l = sb("w0h", [K, D + 2], f32r), sb("w0l", [K, D + 2], f32r)
        w1h, w1l = sb("w1h", [K, H1 * D], f32r), sb("w1l", [K, H1 * D], f32r)
        a1w = sb("a1w", [K, 2, 2 * H1], f32r)
        wout = sb("wout", [H1 * K, D + 2])
        wup, wdown = sb("wup", [K, D]), sb("wdown", [K, D])
        w2h, w2l = sb("w2h", [K, 2 * D], f32r), sb("w2l", [K, 2 * D], f32r)
        wqh, wql = sb("wqh", [K, D], f32r), sb("wql", [K, D], f32r)
        wkh, wkl = sb("wkh", [K, D], f32r), sb("wkl", [K, D], f32r)
        wvh, wvl = sb("wvh", [K, D], f32r), sb("wvl", [K, D], f32r)
        woT = sb("woT", [K, D])
        mask = sb("mask", [T, N])
        adjT = sb("adjT", [T, N], f32r)
        deg = sb("deg", [T])
        linked = sb("linked", [T])
        degb = sb("degb", [T, D])
        ffnb = sb("ffnb", [D])
        gamb, betb, bob = sb("gamb", [D]), sb("betb", [D]), sb("bob", [D])
        bcol = sb("bcol", [4 * K])
        b1c, bqc, bkc, bvc = (bcol[:, K * j:K * j + K] for j in range(4))
        minus_half, zero = sb("minus_half", [T]), sb("zero", [T])

        X = per_slot("X", [T, D])
        HN = per_slot("HN", [T, D])
        HH, HL = per_slot("HH", [K, N], f32r), per_slot("HL", [K, N], f32r)
        ST, MV = per_slot("ST", [T, 6]), per_slot("MV", [T, 2])
        VE, NM, RS, NMR = (per_slot(n, [T]) for n in ("VE", "NM", "RS", "NMR"))
        QK, VAL = [], []
        for s in range(SLOTS):
            with nc.sbuf_tensor(f"QK{s}", [P, 4 * K, N], f32r) as qk:
                QK.append(qk)
            VAL.append(sb(f"VAL{s}", [T, H1 * D]))
        SD = per_slot("SD", [T, 2 * H1])
        NAS = per_slot("NAS", [T, H1])
        SMX = [per_slot(f"SMX{j}_", [T]) for j in range(2)]
        NDM, U, NMX = per_slot("NDM", [T]), per_slot("U", [T]), per_slot("NMX", [T])
        LG = per_slot("LG", [T, N])
        LK = per_slot("LK", [T, N])
        PR = per_slot("PR", [T, N])
        PT = per_slot("PT", [T, N])
        SUM = [per_slot(f"SUM{j}_", [T]) for j in range(2)]
        RI = [per_slot(f"RI{j}_", [T]) for j in range(2)]
        EL = per_slot("EL", [T, D])
        ET = per_slot("ET", [H1 * K, N])
        EX, F1, Y = HN, PT, LK
        MH, ML = HH, HL
        XB1, XB = PR, EL
        OT = [v[:, 0:K, :] for v in ET]
        XO = [v[:, K:2 * K, :] for v in ET]
        SG = [LG, LK]
        QH, QL, KH, KL = ([v[:, j * K:(j + 1) * K, :] for v in QK] for j in range(4))
        VV, O3 = ([v[:, j * K:(j + 1) * K, :] for v in ET] for j in (2, 3))

        def banks(name):
            return [ctx.enter_context(nc.psum_tensor(f"{name}{s}", [P, 512], f32)) for s in range(SLOTS)]
        bankA, bankB = banks("bankA"), banks("bankB")
        AB = [[bankA[s], bankB[s]] for s in range(SLOTS)]

        def s_bank(s, h):
            return AB[s][1 - h % 2]

        def t_bank(s, h):
            return AB[s][1 - h % 2]

        HN_BANK = {LN0: 0, LN1: 1, LN2: 0, LN3: 1}

        def dst_bank(s, g):
            return AB[s][g % 2 if 1 <= g <= H1 else 0]

        def gt_bank(s, g):
            return AB[s][g % 2 if 1 <= g <= H1 else 1]

        def gm_bank(s, g):
            return AB[s][1 - g % 2 if 1 <= g <= H1 else 0]

        def m_bank(s, h):
            return AB[s][h % 2]

        def two(ap):
            return ap[:, :].rearrange("p (t n) -> p t n", t=2)

        w_in = [sem(f"w_in{j}") for j in range(5)]
        set_dve, set_act, set_pool, set_pe = sem("set_dve"), sem("set_act"), sem("set_pool"), sem("set_pe")
        reducing = sem("reducing")
        x_in, stored = sems("x_in"), sems("stored")
        stats, coef_up, normed = sems("stats"), sems("coef_up"), sems("normed")
        turned, hi_up, lo_up = sems("turned"), sems("hi_up"), sems("lo_up")
        dst_up, dmax_up, leak_up, logit_up = (sems(n) for n in ("dst_up", "dmax_up", "leak_up", "logit_up"))
        prob_up, pturned, pvals_up, mixed = sems("prob_up"), sems("pturned"), sems("pvals_up"), sems("mixed")
        rinv_up, score_up, smax_up, o_up = sems("rinv_up"), sems("score_up"), sems("smax_up"), sems("o_up")
        expo_up, elu_up, eturned, eT_up = sems("expo_up"), sems("elu_up"), sems("eturned"), sems("eT_up")
        xb_up, side_up, done = sems("xb_up"), sems("side_up"), sems("done")
        product = sems("product")
        moved = sems("moved")
        taken = sems("taken")

        PROJ0, PROJ1, PARTS, PROJ5, UP, DOWN, MSG, NBR, Q, KEY, V, WO = 1, 2, 6, 7, 8, 9, 10, 11, 12, 13, 14, 15
        PRODUCTS = 15
        M_VAL0, M_VAL1, M_VAL5, M_RELU, M_MSG, M_Q, M_V, M_O, MOVES = 1, 2, 6, 7, 8, 9, 10, 11, 11
        T_SD0, T_SD1, T_SD5, T_MSG, T_OWN, T_QUERY, T_KEY, TAKES = 1, 2, 3, 4, 5, 6, 7, 7

        after = pass_steps()
        starts = {}
        for st in after:
            starts[st] = max([starts[b] + delay(b, st) for b in after[st]], default=0)
        line = sorted(after, key=lambda st: starts[st])
        span = max(starts.values())
        cut = [next(i for i, st in enumerate(line) if starts[st] >= f * span) for f in AHEAD]
        lead_in = interleave(after, [(s, 0, st) for s in range(SLOTS) for st in line[:cut[s]]])
        body = interleave(after, [y for s in range(SLOTS) for y in
                                  [(s, 0, st) for st in line[cut[s]:]] + [(s, 1, st) for st in line[:cut[s]]]])
        lead_out = interleave(after, [(s, 0, st) for s in range(SLOTS) for st in line[cut[s]:]])

        LAST = ITERS - 1

        def walk(eng, handlers):
            def run(order, it):
                for s, late, (name, arg) in order:
                    if name in handlers:
                        handlers[name](s, it + late if late else it, arg)
            run(lead_in, 0)
            with eng.Fori(0, ITERS - 1) as it:
                run(body, it)
            run(lead_out, LAST)

        raw = {n: ET[0][:, 2 * j:2 * j + 2, :] for j, n in enumerate(("Wq", "Wk", "Wv", "Wo"))}
        raw2 = VAL[0][:, 0:2, 0:2 * D]
        raw0 = VAL[0][:, :, 2 * D:3 * D]
        raw1 = VAL[1][:, :, :]
        adji = PR[0][:, :, :].bitcast(i32)
        adjf = PR[1]
        av = ET[1]
        junk = [VAL[s][:, t, c * D:(c + 1) * D] for s in (2, 3) for t in range(T) for c in range(H1)]
        brow = LK[1][:, 0, 0:P]
        a0b = EL[0]
        aOb = EL[1]

        WA, WA1 = sb("WA", [K, 2]), sb("WA1", [K, 2 * H1])
        whole = slice(0, D)
        TURNS = [(adjT, None, whole), (wqh, wql, whole), (wkh, wkl, whole), (wvh, wvl, whole),
                 (w2h, w2l, slice(0, D)), (w2h, w2l, slice(D, 2 * D)), (woT, None, whole)]
        TURN_SRC = [adjf[:, :, :], raw["Wq"], raw["Wk"], raw["Wv"], raw2[:, :, 0:D], raw2[:, :, D:2 * D], raw["Wo"]]
        TURN_BANKS = bankA + bankB[1:]
        A_W0, A_W1, A_TURNS = 1, 2, 3
        w_counts, dve_counts = [], []

        with nc.Block() as block:
            @block.sync
            def _(sp):
                def bc(v):
                    return v.partition_broadcast(P)
                def tiles(w):
                    return w.rearrange("(t p) n -> p t n", p=P)
                g0 = [(adji, tiles(adj)), (raw0, tiles(W0)), (a0b[:, 0, :], bc(a0s)), (a0b[:, 1, :], bc(a0d))]
                g1 = [(raw1[:, :, h * D:(h + 1) * D], tiles(W1[h])) for h in range(H1)]
                g1 += [(av[:, :, :].rearrange("p a n -> p (a n)"), bc(a1.rearrange("h n -> (h n)")))]
                g2 = [(brow[2 * j:2 * j + 2, :], v.rearrange("(t p) -> t p", p=P)) for j, v in enumerate((b1, bq, bk, bv))]
                g2 += [(raw[n], tiles(w)) for n, w in (("Wq", Wq), ("Wk", Wk), ("Wv", Wv), ("Wo", Wo))]
                g2 += [(raw2, tiles(W2))]
                g3 = [(wout[:, :, 0:D], tiles(WO1)), (aOb[:, :, :].rearrange("p a n -> p (a n)"), bc(aO1))]
                g4 = [(degb[:, 0, :], bc(b2g)), (degb[:, 1, :], bc(b2g)), (ffnb[:, :], bc(b2)),
                      (gamb[:, :], bc(gam)), (betb[:, :], bc(bet)), (bob[:, :], bc(bo)),
                      (wup[:, :, :], tiles(w1)), (wdown[:, :, :], tiles(w2))]
                for j, g in enumerate((g0, g1, g2, g3, g4)):
                    for dst, src in g:
                        sp.dma_start(dst, src).then_inc(w_in[j], 16)
                w_counts.extend(16 * len(g) for g in (g0, g1, g2, g3, g4))

                def rows(dram, it, s):
                    return dram[bass.ds(it * SLOTS + s, 1), :, :].rearrange("a (t p) d -> p (a t) d", p=P)

                for s in range(SLOTS):
                    sp.dma_start(X[s][:, :, :], rows(x, 0, s)).then_inc(x_in[s], 16)

                def fetch(s, it, n):
                    if n != LN3 or it is LAST:
                        return
                    sp.wait_ge(xb_up[s], it * 3 + 3)
                    sp.wait_ge(normed[s], it * NLN + NLN)
                    sp.dma_start(X[s][:, :, :], rows(x, it + 1, s)).then_inc(x_in[s], 16)

                def store(s, it, _):
                    sp.wait_ge(done[s], it + 1)
                    sp.dma_start(rows(out, it, s), XO[s]).then_inc(stored[s], 16)

                walk(sp, {"norm": fetch, "done": store})
                for s in range(SLOTS):
                    sp.wait_ge(stored[s], 16 * ITERS + 1)

            @block.gpsimd
            def _(pool):
                pool.memset(ident[:, :], 0.0).then_inc(set_pool, 1)
                pool.memset(minus_half[:, :], -0.5).then_inc(set_pool, 1)
                pool.memset(zero[:, :], 0.0).then_inc(set_pool, 1)
                pool.wait_ge(set_pool, 3)
                pool.affine_select(out=ident[:, :], in_=ident[:, :], compare_op=ALU.not_equal, fill=1.0,
                                   base=0, pattern=[[-1, P]], channel_multiplier=1).then_inc(set_pool, 1)
                pool.wait_ge(w_in[4], w_counts[4])

                def coef(s, it, n):
                    pool.wait_ge(stats[s], it * NLN + n + 1)
                    pool.tensor_tensor(NM[s][:, :], zero[:, :], MV[s][:, :, 0], ALU.subtract)
                    pool.tensor_scalar(VE[s][:, :], MV[s][:, :, 1], EPS, 1.0, ALU.add, ALU.mult)
                    pool.drain()
                    pool.tensor_tensor(RS[s][:, :], VE[s][:, :], minus_half[:, :], ALU.pow)
                    pool.drain()
                    pool.tensor_tensor(NMR[s][:, :], NM[s][:, :], RS[s][:, :], ALU.mult).then_inc(coef_up[s], 1)
                    if n == LN2:
                        add_bias(s, it, 1)
                    if n == LN3:
                        add_bias(s, it, 2)

                def add_bias(s, it, j):
                    dst = XB1[s] if j == 0 else XB[s]
                    for t in range(T):
                        b = (betb[:, :], degb[:, t, :], bob[:, :])[j]
                        ins = pool.tensor_tensor(dst[:, t, :], X[s][:, t, :], b, ALU.add)
                    ins.then_inc(xb_up[s], 1)

                def gb(s, it, _):
                    pool.wait_ge(eturned[s], it + 1)
                    for t in range(T):
                        ins = pool.tensor_tensor(EL[s][:, t, :], EL[s][:, t, :], ffnb[:, :], ALU.add)
                    ins.then_inc(side_up[s], 1)
                    add_bias(s, it, 0)

                def gain(s, it, _):
                    pool.wait_ge(normed[s], it * NLN + LNF + 1)
                    for t in range(T):
                        ins = pool.tensor_tensor(Y[s][:, t, :], HN[s][:, t, :], gamb[:, :], ALU.mult)
                    ins.then_inc(side_up[s], 1)

                walk(pool, {"coef": coef, "gb": gb, "gain": gain})

            @block.scalar
            def _(act):
                act.wait_ge(w_in[0], w_counts[0])
                act.activation(w0h[:, :, 0:D], raw0, ACT.Copy).then_inc(set_act, 1)
                act.wait_ge(w_in[1], w_counts[1])
                act.activation(w1h[:, :, :], raw1, ACT.Copy).then_inc(set_act, 1)
                act.wait_ge(set_pe, 1)
                act.activation(bcol[:, :], bankB[0][:, 0:4 * K], ACT.Copy).then_inc(set_act, 1)
                for n, (hi, lo, cols) in enumerate(TURNS):
                    act.wait_ge(set_pe, n + 2)
                    act.activation(hi[:, :, cols], two(TURN_BANKS[n]), ACT.Copy).then_inc(set_act, 1)

                def norm(s, it, n):
                    act.wait_ge(coef_up[s], it * NLN + n + 1)
                    f = ACT.Identity if n == LNF else ACT.Relu
                    src = Y if n == LNF else X
                    for t in range(T):
                        ins = act.activation(HN[s][:, t, :], src[s][:, t, :], f, bias=NMR[s][:, t:t + 1],
                                             scale=RS[s][:, t:t + 1])
                    ins.then_inc(normed[s], 1)

                def hi(s, it, n):
                    act.wait_ge(turned[s], it * 5 + TURN[n] + 1)
                    act.activation(HH[s][:, :, :], two(AB[s][HN_BANK[n]]), ACT.Copy).then_inc(hi_up[s], 1)

                def vals(s, it, p):
                    act.wait_ge(product[s], it * PRODUCTS + (PROJ5 if p == 5 else PROJ0 + p))
                    if p in (0, 5):
                        for t in range(T):
                            ins = act.activation(VAL[s][:, t, 0:D], AB[s][t][:, 0:D], ACT.Copy)
                    else:
                        t, c = (p - 1) // 2, (p - 1) % 2
                        ins = act.activation(VAL[s][:, t, c * 512:(c + 1) * 512], AB[s][(p - 1) % 2][:, :], ACT.Copy)
                    ins.then_inc(moved[s], 1)

                def leak(s, it, g):
                    act.wait_ge(dmax_up[s], it * GATS + g + 1)
                    h = g - 1 if 1 <= g <= H1 else 0
                    for t in range(T):
                        ins = act.activation(LK[s][:, t, :], LG[s][:, t, :], ACT.Identity,
                                             bias=NAS[s][:, t, h:h + 1], scale=SLOPE[g])
                    ins.then_inc(leak_up[s], 1)

                def prob(s, it, g):
                    act.wait_ge(logit_up[s], it * GATS + g + 1)
                    for t in range(T):
                        ins = act.activation(PR[s][:, t, :], LG[s][:, t, :], ACT.Exp,
                                             bias=NMX[s][:, t:t + 1], scale=-1.0, accum_out=SUM[g % 2][s][:, t:t + 1])
                    ins.then_inc(prob_up[s], 1)

                def sprob(s, it, h):
                    act.wait_ge(smax_up[s], it * H3 + h + 1)
                    r = GATS + h
                    for t in range(T):
                        ins = act.activation(PR[s][:, t, :], SG[h % 2][s][:, t, :], ACT.Exp,
                                             bias=SMX[h % 2][s][:, t:t + 1], scale=-1.0,
                                             accum_out=SUM[r % 2][s][:, t:t + 1])
                    ins.then_inc(prob_up[s], 1)

                def pvals(s, it, r):
                    act.wait_ge(pturned[s], it * ROUNDS + r + 1)
                    bank = gt_bank(s, r) if r < GATS else t_bank(s, r - GATS)
                    act.activation(PT[s][:, :, :], two(bank), ACT.Copy).then_inc(pvals_up[s], 1)

                def expo(s, it, e):
                    g = e + 1
                    if e < H1:
                        act.wait_ge(mixed[s], it * ROUNDS + g + 1)
                        ins = act.activation(EX[s][:, :, :], two(gm_bank(s, g)), ACT.Exp)
                    else:
                        act.wait_ge(rinv_up[s], it * ROUNDS + g + 1)
                        act.wait_ge(mixed[s], it * ROUNDS + g + 1)
                        for t in range(T):
                            ins = act.activation(EX[s][:, t, :], bankA[s][:, t * D:(t + 1) * D], ACT.Exp,
                                                 scale=RI[g % 2][s][:, t:t + 1])
                    ins.then_inc(expo_up[s], 1)

                def relu(s, it, _):
                    act.wait_ge(product[s], it * PRODUCTS + UP)
                    for t in range(K):
                        ins = act.activation(F1[s][:, t, :], bankA[s][:, t * N:(t + 1) * N], ACT.Relu, bias=b1c[:, t:t + 1])
                    ins.then_inc(moved[s], 1)

                def mhi(s, it, _):
                    act.wait_ge(product[s], it * PRODUCTS + MSG)
                    for t in range(T):
                        ins = act.activation(MH[s][:, t, :], AB[s][t][:, D:2 * D], ACT.Copy)
                    ins.then_inc(moved[s], 1)

                def qs(s, it, _):
                    act.wait_ge(product[s], it * PRODUCTS + Q)
                    for t in range(K):
                        ins = act.activation(QH[s][:, t, :], bankA[s][:, t * N:(t + 1) * N], ACT.Identity,
                                             bias=bqc[:, t:t + 1])
                    ins.then_inc(moved[s], 1)

                def vs(s, it, _):
                    act.wait_ge(product[s], it * PRODUCTS + V)
                    act.activation(VV[s], two(bankA[s]), ACT.Copy).then_inc(moved[s], 1)

                def oT(s, it, _):
                    act.wait_ge(turned[s], it * 5 + 5)
                    act.activation(OT[s], two(bankA[s]), ACT.Copy).then_inc(moved[s], 1)

                walk(act, {"norm": norm, "hi": hi, "vals": vals, "leak": leak, "prob": prob, "sprob": sprob,
                           "pvals": pvals, "spvals": lambda s, it, h: pvals(s, it, GATS + h), "expo": expo,
                           "relu": relu, "mhi": mhi, "qs": qs, "vs": vs, "oT": oT})

            @block.vector
            def _(dve):
                count = [0]

                def mark(ins):
                    count[0] += 1
                    ins.then_inc(set_dve, 1)

                dve.wait_ge(w_in[0], w_counts[0])
                mark(dve.tensor_copy(adjf[:, :, :], adji))
                dve.wait_ge(set_dve, count[0])
                mark(dve.tensor_scalar(mask[:, :, :], adjf[:, :, :], 0.0, MASKED, ALU.is_equal, ALU.mult))
                mark(dve.tensor_reduce(deg[:, :], adjf[:, :, :], AX.X, ALU.add))
                dve.wait_ge(set_dve, count[0])
                mark(dve.tensor_reduce(linked[:, :], adjf[:, :, :], AX.X, ALU.max))
                def dots(terms):
                    for row, (dst, rows, vec) in zip(junk, terms):
                        dve.tensor_tensor_reduce(out=row, in0=rows, in1=vec, scale=1.0, scalar=0.0,
                                                 op0=ALU.mult, op1=ALU.add, accum_out=dst)
                    dve.drain()

                dots([(WA[:, t, j:j + 1], raw0[:, t, :], a0b[:, j, :]) for t in range(K) for j in range(2)])
                mark(dve.tensor_copy(w0h[:, :, D:D + 2], WA[:, :, :]))
                dve.wait_ge(set_act, A_W0)
                mark(dve.tensor_tensor(w0l[:, :, 0:D], raw0, w0h[:, :, 0:D].bitcast(f32), ALU.subtract))
                dve.wait_ge(set_dve, count[0])
                mark(dve.tensor_tensor(w0l[:, :, D:D + 2], WA[:, :, :], w0h[:, :, D:D + 2].bitcast(f32), ALU.subtract))
                dve.wait_ge(w_in[1], w_counts[1])
                dots([(WA1[:, t, j * H1 + h:j * H1 + h + 1], raw1[:, t, h * D:(h + 1) * D], av[:, 2 * h + j, :])
                      for t in range(K) for j in range(2) for h in range(H1)])
                mark(dve.tensor_copy(a1w[:, :, 0, :], WA1[:, :, :]))
                dve.wait_ge(set_act, A_W1)
                mark(dve.tensor_tensor(w1l[:, :, :], raw1, w1h[:, :, :].bitcast(f32), ALU.subtract))
                dve.wait_ge(set_dve, count[0])
                mark(dve.tensor_tensor(a1w[:, :, 1, :], WA1[:, :, :], a1w[:, :, 0, :].bitcast(f32), ALU.subtract))
                for n, (hi, lo, cols) in enumerate(TURNS):
                    if lo is not None:
                        dve.wait_ge(set_act, A_TURNS + n + 1)
                        mark(dve.tensor_tensor(lo[:, :, cols], two(TURN_BANKS[n]), hi[:, :, cols].bitcast(f32),
                                               ALU.subtract))
                dve.wait_ge(w_in[3], w_counts[3])
                dots([(wout[:, t, D + j:D + j + 1], wout[:, t, 0:D], aOb[:, j, :]) for t in range(H1 * K) for j in range(2)])
                dve.wait_ge(w_in[4], w_counts[4])
                for t in range(T):
                    mark(dve.tensor_scalar(degb[:, t, :], degb[:, t, :], deg[:, t:t + 1], None, ALU.mult))
                mark(dve.tensor_scalar(ffnb[:, :], ffnb[:, :], -1.0, None, ALU.add))
                dve.wait_ge(set_pe, len(TURNS) + 2)
                mark(dve.tensor_tensor(bob[:, :], bankB[0][:, D:2 * D], bob[:, :], ALU.add))
                dve_counts.append(count[0])

                def stats_(s, it, n):
                    if n == LN0:
                        dve.wait_ge(x_in[s], it * 16 + 16)
                    src = Y if n == LNF else X
                    for t in range(T):
                        dve.bn_stats(ST[s][:, t, :], src[s][:, t, :])
                    dve.drain()
                    for t in range(T):
                        ins = dve.bn_aggr(MV[s][:, t, :], ST[s][:, t, :])
                    ins.then_inc(stats[s], 1)

                def lo(s, it, n):
                    dve.wait_ge(hi_up[s], it * 4 + TURN[n] + 1)
                    dve.tensor_tensor(HL[s][:, :, :], two(AB[s][HN_BANK[n]]), HH[s][:, :, :].bitcast(f32),
                                      ALU.subtract).then_inc(lo_up[s], 1)

                def sd(s, it, l):
                    heads = H1 if l == 1 else 1
                    if l == 1:
                        dve.wait_ge(product[s], it * PRODUCTS + PARTS)
                        halves = bankA[s][:, 0:8 * H1].rearrange("p (t a n) -> p t a n", t=T, a=2)
                        dve.tensor_copy(SD[s][:, :, :], halves[:, :, 1, :])
                        dve.drain()
                        dve.tensor_tensor(SD[s][:, :, :], halves[:, :, 0, :], SD[s][:, :, :], ALU.add)
                    else:
                        dve.wait_ge(moved[s], it * MOVES + (M_VAL5 if l else M_VAL0))
                        for t in range(T):
                            dve.tensor_copy(SD[s][:, t, 0:2], AB[s][t][:, D:D + 2])
                    dve.drain()
                    dve.tensor_scalar(NAS[s][:, :, 0:heads], SD[s][:, :, 0:heads], -SLOPE[l], None,
                                      ALU.mult).then_inc(taken[s], 1)

                def dmax(s, it, g):
                    dve.wait_ge(dst_up[s], it * GATS + g + 1)
                    if g:
                        dve.wait_ge(prob_up[s], it * ROUNDS + g)
                    h = g - 1 if 1 <= g <= H1 else 0
                    dve.sem_inc(reducing, 1)
                    for t in range(T):
                        ins = dve.tensor_tensor_reduce(out=LG[s][:, t, :], in0=dst_bank(s, g)[:, 0:N], in1=mask[:, t, :],
                                                       scale=-1.0, scalar=3.0e38, op0=ALU.add, op1=ALU.min,
                                                       accum_out=NDM[s][:, t:t + 1])
                    ins.then_inc(dmax_up[s], 1)
                    dve.drain()
                    dve.tensor_tensor(U[s][:, :], NDM[s][:, :], SD[s][:, :, h], ALU.subtract)
                    dve.drain()
                    dve.scalar_tensor_tensor(NMX[s][:, :], U[s][:, :], SLOPE[g], U[s][:, :], ALU.mult, ALU.min)

                def logit(s, it, g):
                    dve.wait_ge(leak_up[s], it * GATS + g + 1)
                    h = g - 1 if 1 <= g <= H1 else 0
                    for t in range(T):
                        ins = dve.scalar_tensor_tensor(LG[s][:, t, :], LG[s][:, t, :], SD[s][:, t, h:h + 1],
                                                       LK[s][:, t, :], ALU.subtract, ALU.min)
                    ins.then_inc(logit_up[s], 1)

                def rinv(s, it, r):
                    dve.wait_ge(prob_up[s], it * ROUNDS + r + 1)
                    ins = dve.reciprocal(RI[r % 2][s][:, :], SUM[r % 2][s][:, :])
                    if r == 0:
                        dve.drain()
                        ins = dve.tensor_tensor(RI[0][s][:, :], RI[0][s][:, :], linked[:, :], ALU.mult)
                    ins.then_inc(rinv_up[s], 1)

                def x0(s, it, _):
                    dve.wait_ge(rinv_up[s], it * ROUNDS + 1)
                    dve.wait_ge(mixed[s], it * ROUNDS + 1)
                    for t in range(T):
                        ins = dve.scalar_tensor_tensor(X[s][:, t, :], bankA[s][:, t * D:(t + 1) * D], RI[0][s][:, t:t + 1],
                                                       X[s][:, t, :], ALU.mult, ALU.add)
                    dve.drain()

                def pnorm(s, it, g):
                    dve.wait_ge(prob_up[s], it * ROUNDS + g + 1)
                    dve.reciprocal(RI[g % 2][s][:, :], SUM[g % 2][s][:, :])
                    dve.drain()
                    for t in range(T):
                        ins = dve.tensor_scalar(PR[s][:, t, :], PR[s][:, t, :], RI[g % 2][s][:, t:t + 1], None, ALU.mult)
                    ins.then_inc(rinv_up[s], 1)

                def elu(s, it, e):
                    g = e + 1
                    if e == 1:
                        dve.wait_ge(stored[s], it * 16 + 1)
                    dve.wait_ge(expo_up[s], it * (H1 + 1) + e + 1)
                    if e < H1:
                        dve.tensor_scalar(EL[s][:, :, :], EX[s][:, :, :], 1.0, -1.0, ALU.min, ALU.add)
                        dve.drain()
                        dve.scalar_tensor_tensor(ET[s][:, 2 * e:2 * e + 2, :], two(gm_bank(s, g)), 0.0, EL[s][:, :, :],
                                                 ALU.max, ALU.add).then_inc(elu_up[s], 1)
                    else:
                        for t in range(T):
                            dve.tensor_scalar(EL[s][:, t, :], bankA[s][:, t * D:(t + 1) * D], RI[g % 2][s][:, t:t + 1],
                                              0.0, ALU.mult, ALU.max)
                        dve.drain()
                        dve.scalar_tensor_tensor(EL[s][:, :, :], EX[s][:, :, :], 1.0, EL[s][:, :, :], ALU.min,
                                                 ALU.add).then_inc(elu_up[s], 1)

                def eT(s, it, e):
                    dve.wait_ge(eturned[s], it + 1)
                    dve.tensor_scalar(OT[s], two(bankB[s]), -1.0, None, ALU.add).then_inc(eT_up[s], 1)

                def ysum(s, it, _):
                    dve.wait_ge(side_up[s], it * 2 + 1)
                    dve.wait_ge(product[s], it * PRODUCTS + DOWN)
                    dve.tensor_tensor(Y[s][:, :, :], two(bankB[s]), EL[s][:, :, :], ALU.add)
                    dve.drain()

                def x1(s, it, _):
                    dve.wait_ge(xb_up[s], it * 3 + 1)
                    dve.wait_ge(side_up[s], it * 2 + 2)
                    dve.tensor_tensor(X[s][:, :, :], Y[s][:, :, :], XB1[s][:, :, :], ALU.add)
                    dve.drain()

                def mlo(s, it, _):
                    dve.wait_ge(moved[s], it * MOVES + M_MSG)
                    for t in range(T):
                        ins = dve.tensor_tensor(ML[s][:, t, :], AB[s][t][:, D:2 * D], MH[s][:, t, :].bitcast(f32),
                                                ALU.subtract)
                    ins.then_inc(taken[s], 1)

                def own(s, it, _):
                    dve.wait_ge(xb_up[s], it * 3 + 2)
                    for t in range(T):
                        ins = dve.scalar_tensor_tensor(X[s][:, t, :], AB[s][t][:, 0:D], deg[:, t:t + 1],
                                                       XB[s][:, t, :], ALU.mult, ALU.add)
                    ins.then_inc(taken[s], 1)
                    dve.drain()

                def x2(s, it, _):
                    dve.wait_ge(product[s], it * PRODUCTS + NBR)
                    dve.tensor_tensor(X[s][:, :, :], two(bankA[s]), X[s][:, :, :], ALU.add)
                    dve.drain()

                def ks(s, it, _):
                    dve.wait_ge(product[s], it * PRODUCTS + KEY)
                    for t in range(K):
                        dve.tensor_scalar(KH[s][:, t, :], bankB[s][:, t * N:(t + 1) * N], bkc[:, t:t + 1], None, ALU.add)

                def qlo(s, it, _):
                    dve.wait_ge(moved[s], it * MOVES + M_Q)
                    for t in range(K):
                        ins = dve.scalar_tensor_tensor(QL[s][:, t, :], bankA[s][:, t * N:(t + 1) * N], bqc[:, t:t + 1],
                                                       QH[s][:, t, :].bitcast(f32), ALU.add, ALU.subtract)
                    ins.then_inc(taken[s], 1)

                def klo(s, it, _):
                    dve.drain()
                    for t in range(K):
                        ins = dve.scalar_tensor_tensor(KL[s][:, t, :], bankB[s][:, t * N:(t + 1) * N], bkc[:, t:t + 1],
                                                       KH[s][:, t, :].bitcast(f32), ALU.add, ALU.subtract)
                    ins.then_inc(taken[s], 1)

                def smax(s, it, h):
                    dve.wait_ge(score_up[s], it * H3 + h + 1)
                    if h >= 2:
                        dve.wait_ge(prob_up[s], it * ROUNDS + GATS + h - 1)
                    dve.sem_inc(reducing, 1)
                    for t in range(T):
                        ins = dve.tensor_tensor_reduce(out=SG[h % 2][s][:, t, :], in0=s_bank(s, h)[:, t * N:(t + 1) * N],
                                                       in1=mask[:, t, :], scale=-SCALE, scalar=3.0e38, op0=ALU.add,
                                                       op1=ALU.min, accum_out=SMX[h % 2][s][:, t:t + 1])
                    ins.then_inc(smax_up[s], 1)

                def onorm(s, it, h):
                    r = GATS + h
                    dve.wait_ge(rinv_up[s], it * ROUNDS + r + 1)
                    dve.wait_ge(mixed[s], it * ROUNDS + r + 1)
                    for t in range(T):
                        ins = dve.tensor_scalar(O3[s][:, t, h * DH:(h + 1) * DH], m_bank(s, h)[:, t * DH:(t + 1) * DH],
                                                RI[r % 2][s][:, t:t + 1], None, ALU.mult)
                    ins.then_inc(o_up[s], 1)

                def finish(s, it, _):
                    dve.wait_ge(xb_up[s], it * 3 + 3)
                    dve.wait_ge(product[s], it * PRODUCTS + WO)
                    dve.tensor_tensor(XO[s], two(bankB[s]), XB[s][:, :, :], ALU.add).then_inc(done[s], 1)

                for s in range(SLOTS):
                    dve.sem_inc(stored[s], 1)
                walk(dve, {"stats": stats_, "lo": lo, "sd": sd, "dmax": dmax, "logit": logit, "rinv": rinv,
                           "pnorm": pnorm, "x0": x0, "elu": elu, "eT": eT, "ysum": ysum, "x1": x1, "mlo": mlo, "self": own, "x2": x2,
                           "ks": ks, "qlo": qlo, "klo": klo, "smax": smax, "onorm": onorm, "done": finish})

            @block.tensor
            def _(pe):
                pe.wait_ge(set_pool, 4)
                pe.wait_ge(w_in[2], w_counts[2])
                pe.transpose(bankB[0][:, 0:4 * K], brow[0:4 * K, :], ident[0:4 * K, 0:4 * K]).then_inc(set_pe, 1)
                pe.wait_ge(set_dve, 1)
                for n in range(len(TURNS)):
                    for k in range(K):
                        for t in range(2):
                            last = pe.transpose(TURN_BANKS[n][:, k * 256 + t * P:k * 256 + (t + 1) * P],
                                                TURN_SRC[n][:, t, k * P:(k + 1) * P], ident[:, :])
                    last.then_inc(set_pe, 1)
                pe.wait_ge(set_act, A_TURNS + len(TURNS))
                for k in range(K):
                    last = pe.matmul(bankB[0][:, D:2 * D], bvc[:, k:k + 1].to_broadcast([P, P]), woT[:, k, :],
                                     start=(k == 0), stop=(k == K - 1))
                last.then_inc(set_pe, 1)
                pe.wait_ge(set_dve, dve_counts[0])
                pe.wait_ge(w_in[4], w_counts[4])

                def three(bank, stat, mov):
                    ops = [(k, a, b) for k in range(K) for a, b in ((0, 0), (0, 1), (1, 0))]
                    for n, (k, a, b) in enumerate(ops):
                        last = pe.matmul(bank, stat(a, k), mov(b, k), start=(n == 0), stop=(n == len(ops) - 1))
                    return last

                def turn(s, it, n):
                    pe.wait_ge(normed[s], it * NLN + n + 1)
                    for k in range(K):
                        for t in range(T):
                            last = pe.transpose(AB[s][HN_BANK[n]][:, k * N + t * P:k * N + (t + 1) * P],
                                                HN[s][:, t, k * P:(k + 1) * P], ident[:, :])
                    last.then_inc(turned[s], 1)

                def h_tile(s, t):
                    return lambda a, k: (HH, HL)[a][s][:, k, t * P:(t + 1) * P]

                def h_all(s):
                    return lambda a, k: (HH, HL)[a][s][:, k, :]

                def proj(s, it, p):
                    if p == 0:
                        pe.wait_ge(lo_up[s], it * 4 + 1)
                        for t in range(T):
                            last = three(AB[s][t][:, 0:D + 2], h_tile(s, t), lambda b, k: (w0h, w0l)[b][:, k, :])
                    elif p == 5:
                        pe.wait_ge(elu_up[s], it * (H1 + 1) + H1)
                        for t in range(T):
                            for k in range(H1 * K):
                                last = pe.matmul(AB[s][t][:, 0:D + 2], ET[s][:, k, t * P:(t + 1) * P], wout[:, k, :],
                                                 start=(k == 0), stop=(k == H1 * K - 1))
                    else:
                        if p == 1:
                            pe.wait_ge(lo_up[s], it * 4 + 2)
                        if p > 2:
                            pe.wait_ge(moved[s], it * MOVES + M_VAL1 + p - 3)
                        t, c = (p - 1) // 2, (p - 1) % 2
                        last = three(AB[s][(p - 1) % 2][:, :], h_tile(s, t),
                                     lambda b, k: (w1h, w1l)[b][:, k, c * 512:(c + 1) * 512])
                    last.then_inc(product[s], 1)

                def sdp(s, it, _):
                    pe.wait_ge(moved[s], it * MOVES + M_VAL1 + 2)
                    for t in range(T):
                        c = t * 4 * H1
                        for k in range(K):
                            pe.matmul(bankA[s][:, c:c + 4 * H1], h_tile(s, t)(0, k),
                                      a1w[:, k, :, :].rearrange("p a b -> p (a b)"), start=(k == 0), stop=False)
                            last = pe.matmul(bankA[s][:, c:c + 2 * H1], h_tile(s, t)(1, k), a1w[:, k, 0, :],
                                             start=False, stop=(k == K - 1))
                    last.then_inc(product[s], 1)

                def dst(s, it, g):
                    pe.wait_ge(taken[s], it * TAKES + (T_SD0 if g == 0 else T_SD5 if g == 5 else T_SD1))
                    if g == 1:
                        pe.wait_ge(moved[s], it * MOVES + M_VAL1 + 3)
                    if 3 <= g <= H1:
                        pe.wait_ge(pvals_up[s], it * ROUNDS + g - 1)
                    c = H1 + g - 1 if 1 <= g <= H1 else 1
                    for t in range(T):
                        last = pe.transpose(dst_bank(s, g)[:, t * P:(t + 1) * P], SD[s][:, t, c:c + 1].to_broadcast([P, P]),
                                            ident[:, :])
                    last.then_inc(dst_up[s], 1)

                def pturn(s, it, r):
                    pe.wait_ge(rinv_up[s] if 1 <= r <= H1 else prob_up[s], it * ROUNDS + r + 1)
                    bank = gt_bank(s, r) if r < GATS else t_bank(s, r - GATS)
                    if 2 <= r <= H1:
                        pe.wait_ge(elu_up[s], it * (H1 + 1) + r - 1)
                    if r > GATS:
                        pe.wait_ge(o_up[s], it * H3 + r - GATS)
                    for j in range(T):
                        for t in range(T):
                            last = pe.transpose(bank[:, j * N + t * P:j * N + (t + 1) * P],
                                                PR[s][:, t, j * P:(j + 1) * P], ident[:, :])
                    last.then_inc(pturned[s], 1)

                def mix(s, it, g):
                    pe.wait_ge(pvals_up[s], it * ROUNDS + g + 1)
                    if 1 <= g < H1:
                        pe.wait_ge(dmax_up[s], it * GATS + g + 2)
                    for t in range(T):
                        for j in range(T):
                            if 1 <= g <= H1:
                                c = (g - 1) * D + t * P
                                last = pe.matmul(gm_bank(s, g)[:, t * N:(t + 1) * N], VAL[s][:, j, c:c + P],
                                                 PT[s][:, j, :], start=(j == 0), stop=(j == T - 1))
                            else:
                                last = pe.matmul(bankA[s][:, t * D:(t + 1) * D], PT[s][:, j, t * P:(t + 1) * P],
                                                 VAL[s][:, j, 0:D], start=(j == 0), stop=(j == T - 1))
                    last.then_inc(mixed[s], 1)

                def eturn(s, it, e):
                    pe.wait_ge(elu_up[s], it * (H1 + 1) + H1 + 1)
                    for k in range(K):
                        for t in range(T):
                            last = pe.transpose(bankB[s][:, k * N + t * P:k * N + (t + 1) * P],
                                                EL[s][:, t, k * P:(k + 1) * P], ident[:, :])
                    last.then_inc(eturned[s], 1)

                def up(s, it, _):
                    pe.wait_ge(eT_up[s], it + 1)
                    for t in range(K):
                        for k in range(K):
                            last = pe.matmul(bankA[s][:, t * N:(t + 1) * N], wup[:, k, t * P:(t + 1) * P], OT[s][:, k, :],
                                             start=(k == 0), stop=(k == K - 1))
                    last.then_inc(product[s], 1)

                def down(s, it, _):
                    pe.wait_ge(moved[s], it * MOVES + M_RELU)
                    for t in range(T):
                        for k in range(K):
                            last = pe.matmul(bankB[s][:, t * D:(t + 1) * D], F1[s][:, k, t * P:(t + 1) * P], wdown[:, k, :],
                                             start=(k == 0), stop=(k == K - 1))
                    last.then_inc(product[s], 1)

                def msg(s, it, _):
                    pe.wait_ge(lo_up[s], it * 4 + 3)
                    for t in range(T):
                        last = three(AB[s][t][:, :], h_tile(s, t), lambda b, k: (w2h, w2l)[b][:, k, :])
                    last.then_inc(product[s], 1)

                def nbr(s, it, _):
                    pe.wait_ge(taken[s], it * TAKES + T_OWN)
                    for t in range(T):
                        ops = [(j, m) for j in range(T) for m in (MH, ML)]
                        for n, (j, m) in enumerate(ops):
                            last = pe.matmul(bankA[s][:, t * D:(t + 1) * D], adjT[:, j, t * P:(t + 1) * P], m[s][:, j, :],
                                             start=(n == 0), stop=(n == len(ops) - 1))
                    last.then_inc(product[s], 1)

                def q(s, it, _):
                    pe.wait_ge(lo_up[s], it * 4 + 4)
                    for t in range(K):
                        last = three(bankA[s][:, t * N:(t + 1) * N],
                                     lambda a, k: (wqh, wql)[a][:, k, t * P:(t + 1) * P], h_all(s))
                    last.then_inc(product[s], 1)

                def k_(s, it, _):
                    for t in range(K):
                        last = three(bankB[s][:, t * N:(t + 1) * N],
                                     lambda a, k: (wkh, wkl)[a][:, k, t * P:(t + 1) * P], h_all(s))
                    last.then_inc(product[s], 1)

                def v(s, it, _):
                    pe.wait_ge(taken[s], it * TAKES + T_QUERY)
                    for t in range(T):
                        last = three(bankA[s][:, t * D:(t + 1) * D], h_tile(s, t), lambda b, k: (wvh, wvl)[b][:, k, :])
                    last.then_inc(product[s], 1)

                def score(s, it, h):
                    if h == 0:
                        pe.wait_ge(taken[s], it * TAKES + T_KEY)
                    elif h == 1:
                        pe.wait_ge(moved[s], it * MOVES + M_V)
                    else:
                        pe.wait_ge(pvals_up[s], it * ROUNDS + GATS + h - 1)
                    o, r = (h * DH) // P, (h * DH) % P
                    for t in range(T):
                        for n, (a, b) in enumerate(((QH, KH), (QH, KL), (QL, KH))):
                            last = pe.matmul(s_bank(s, h)[:, t * N:(t + 1) * N], a[s][r:r + DH, o, t * P:(t + 1) * P],
                                             b[s][r:r + DH, o, :], start=(n == 0), stop=(n == 2))
                    last.then_inc(score_up[s], 1)

                def spturn(s, it, h):
                    pturn(s, it, GATS + h)

                def smix(s, it, h):
                    pe.wait_ge(pvals_up[s], it * ROUNDS + GATS + h + 1)
                    if h + 1 < H3:
                        pe.wait_ge(smax_up[s], it * H3 + h + 2)
                    for t in range(T):
                        for j in range(T):
                            last = pe.matmul(m_bank(s, h)[:, t * DH:(t + 1) * DH], PT[s][:, j, t * P:(t + 1) * P],
                                             VV[s][:, j, h * DH:(h + 1) * DH], start=(j == 0), stop=(j == T - 1))
                    last.then_inc(mixed[s], 1)

                def oturn(s, it, _):
                    pe.wait_ge(o_up[s], it * H3 + H3)
                    for k in range(K):
                        for t in range(T):
                            last = pe.transpose(bankA[s][:, k * N + t * P:k * N + (t + 1) * P],
                                                O3[s][:, t, k * P:(k + 1) * P], ident[:, :])
                    last.then_inc(turned[s], 1)

                def wo(s, it, _):
                    pe.wait_ge(moved[s], it * MOVES + M_O)
                    for t in range(T):
                        for k in range(K):
                            last = pe.matmul(bankB[s][:, t * D:(t + 1) * D], OT[s][:, k, t * P:(t + 1) * P], woT[:, k, :],
                                             start=(k == 0), stop=(k == K - 1))
                    last.then_inc(product[s], 1)

                walk(pe, {"turn": turn, "proj": proj, "sdp": sdp, "dst": dst, "pturn": pturn, "mix": mix,
                          "eturn": eturn, "up": up, "down": down, "msg": msg, "nbr": nbr, "q": q, "k": k_, "v": v,
                          "score": score, "spturn": spturn, "smix": smix, "oturn": oturn, "wo": wo})


_INS = ['x', 'adj', 'L0_gnn_W', 'L0_gnn_a_src', 'L0_gnn_a_dst', 'L1_gnn_W_heads', 'L1_gnn_a_heads', 'L1_gnn_W_out',
        'L1_gnn_a_out', 'L1_gnn_w1', 'L1_gnn_b1', 'L1_gnn_w2', 'L1_gnn_b2', 'L1_gnn_ln_gamma', 'L1_gnn_ln_beta',
        'L2_gnn_W', 'L2_gnn_b', 'L3_gnn_Wq', 'L3_gnn_bq', 'L3_gnn_Wk', 'L3_gnn_bk', 'L3_gnn_Wv', 'L3_gnn_bv',
        'L3_gnn_Wo', 'L3_gnn_bo']


def kernel(**inputs):
    import numpy as _np
    import concourse.bacc as _bacc
    from concourse import mybir as _mybir
    from concourse.bass_utils import run_bass_kernel_spmd as _run

    nc = _bacc.Bacc("TRN2", target_bir_lowering=False, num_devices=1)
    arrays, args = {}, []
    for name in _INS:
        a = _np.ascontiguousarray(inputs[name])
        arrays[f"in_{name}"] = a
        args.append(nc.dram_tensor(f"in_{name}", a.shape, _mybir.dt.from_np(a.dtype), kind="ExternalInput").ap())
    out = nc.dram_tensor("out_dram", (NB, N, D), _mybir.dt.float32, kind="ExternalOutput").ap()
    build(nc, *args, out)
    r = _run(nc, [arrays], core_ids=[0])
    return r.results[0]["out_dram"]
```
